# Optimizing a Trainium2 kernel written in Bass

```python
import numpy as np
import jax
import jax.numpy as jnp

def _softmax(x, axis=-1):
    return jax.nn.softmax(x, axis=axis)

def _gelu(x):
    return jax.nn.gelu(x, approximate=True)

def _silu(x):
    return jax.nn.silu(x)

def _sigmoid(x):
    return jax.nn.sigmoid(x)

def _layernorm(x, axis=-1, eps=1e-05):
    m = jnp.mean(x, axis=axis, keepdims=True)
    v = jnp.var(x, axis=axis, keepdims=True)
    return (x - m) / jnp.sqrt(v + eps)

def _scatter_add(tgt, idx, src, axis=0):
    return tgt.at[idx].add(src)

def _segment_sum(src, seg, n):
    return jax.ops.segment_sum(src, seg, n)
kernel_name = 'mk_seq_postln_d1_jaxref_r8_cdbf9e'

def setup_inputs(seed: int=0):
    np.random.seed(seed)
    _w = jnp.asarray

    def _L0_attn_setup():
        import jax, jax.numpy as jnp
        import numpy as np
        N_HEADS = 16
        HEAD_DIM = 64
        DIM = 128
        BATCH = 2
        SEQ = 256
        key = jax.random.key(seed)
        ks = jax.random.split(key, 6)
        hd = N_HEADS * HEAD_DIM
        scale_in = 1.0 / np.sqrt(DIM)
        scale_out = 1.0 / np.sqrt(hd)
        return {'x': jax.random.normal(ks[0], (BATCH, SEQ, DIM), dtype=jnp.float32), 'Wq': jax.random.normal(ks[1], (DIM, hd), dtype=jnp.float32) * scale_in, 'Wk': jax.random.normal(ks[2], (DIM, hd), dtype=jnp.float32) * scale_in, 'Wv': jax.random.normal(ks[3], (DIM, hd), dtype=jnp.float32) * scale_in, 'Wo': jax.random.normal(ks[4], (hd, DIM), dtype=jnp.float32) * scale_out, 'bo': jnp.zeros((DIM,), dtype=jnp.float32)}
    _L0_attn_in = _L0_attn_setup()

    def _L0_ffn_setup():
        import jax, jax.numpy as jnp
        import numpy as np
        TOP_K = 2
        key = jax.random.key(seed)
        k1, k2, k3, k4 = jax.random.split(key, 4)
        B, S, H, F, E = (2, 256, 128, 352, 8)
        hidden_states = jax.random.normal(k1, (B, S, H), dtype=jnp.float32)
        wqkv = jax.random.normal(k2, (3 * E, H), dtype=jnp.float32) * 0.02
        w1 = jax.random.normal(k3, (E, 2 * F, H), dtype=jnp.float32) * 0.02
        w2 = jax.random.normal(k4, (E, H, F), dtype=jnp.float32) * 0.02
        return {'hidden_states': hidden_states, 'wqkv': wqkv, 'w1': w1, 'w2': w2}
    _L0_ffn_in = _L0_ffn_setup()
    _d = {'L0_attn_x': _L0_attn_in['x'], 'L0_attn_Wq': _L0_attn_in['Wq'], 'L0_attn_Wk': _L0_attn_in['Wk'], 'L0_attn_Wv': _L0_attn_in['Wv'], 'L0_attn_Wo': _L0_attn_in['Wo'], 'L0_attn_bo': _L0_attn_in['bo'], 'L0_ffn_wqkv': _L0_ffn_in['wqkv'], 'L0_ffn_w1': _L0_ffn_in['w1'], 'L0_ffn_w2': _L0_ffn_in['w2']}
    _x0 = _d['L0_attn_x']
    _d['L0_attn_x'] = jax.random.normal(jax.random.fold_in(jax.random.key(seed), 1), (2, 1024, 128), dtype=_x0.dtype)
    del _x0
    return _d

def reference(L0_attn_x, L0_attn_Wq, L0_attn_Wk, L0_attn_Wv, L0_attn_Wo, L0_attn_bo, L0_ffn_wqkv, L0_ffn_w1, L0_ffn_w2):

    def _L0_attn_ref(x, Wq, Wk, Wv, Wo, bo):
        import jax, jax.numpy as jnp
        import numpy as np
        N_HEADS = 16
        HEAD_DIM = 64
        DIM = 128
        BATCH = 2
        SEQ = 256
        b, s, _ = x.shape
        q = (x @ Wq).reshape(b, s, N_HEADS, HEAD_DIM)
        k = (x @ Wk).reshape(b, s, N_HEADS, HEAD_DIM)
        v = (x @ Wv).reshape(b, s, N_HEADS, HEAD_DIM)
        dot = jnp.einsum('bihd,bkhd->bhik', q, k)
        w = jax.nn.softmax(dot / jnp.sqrt(jnp.float32(HEAD_DIM)), axis=-1)
        a = jnp.einsum('bhij,bjhd->bihd', w, v)
        a = a.reshape(b, s, N_HEADS * HEAD_DIM)
        return a @ Wo + bo

    def _L0_ffn_ref(hidden_states, wqkv, w1, w2):
        import jax, jax.numpy as jnp
        import numpy as np
        TOP_K = 2
        b, s, h = hidden_states.shape
        E = w1.shape[0]
        mixed = hidden_states @ wqkv.T
        q, k, v = jnp.split(mixed, 3, axis=-1)
        q = q.astype(jnp.float32)
        k = k.astype(jnp.float32)
        v = v.astype(jnp.float32)
        attn = jax.nn.softmax(q[..., :, None] * k[..., None, :], axis=-1)
        logits = jnp.einsum('bsej,bsj->bse', attn, v).reshape(-1, E)
        top_logits, idx = jax.lax.top_k(logits, TOP_K)
        scores = jax.nn.softmax(top_logits.astype(jnp.float32), axis=-1).astype(hidden_states.dtype)
        N = b * s
        x = hidden_states.reshape(N, h)
        token_ids = jnp.repeat(jnp.arange(N), TOP_K)
        expert_ids = idx.reshape(-1)
        x_rep = x[token_ids]
        out = jnp.zeros_like(x_rep)
        for e in range(E):
            h1 = x_rep @ w1[e].T
            a, g = jnp.split(h1, 2, axis=-1)
            he = jax.nn.silu(a) * g @ w2[e].T
            out = out + jnp.where((expert_ids == e)[:, None], he, jnp.zeros((), out.dtype))
        out = out * scores.reshape(-1, 1)
        combined = out.reshape(N, TOP_K, h).sum(axis=1)
        return combined.reshape(b, s, h)
    x = L0_attn_x
    x = _layernorm(x + _L0_attn_ref(x, L0_attn_Wq, L0_attn_Wk, L0_attn_Wv, L0_attn_Wo, L0_attn_bo), axis=-1)
    x = _layernorm(x + _L0_ffn_ref(x, L0_ffn_wqkv, L0_ffn_w1, L0_ffn_w2), axis=-1)
    return x

_drawn_inputs = setup_inputs


def setup_inputs(seed=0):
    import zlib

    import numpy as np

    out = dict(_drawn_inputs(seed))
    spreads = {'L0_attn_bo': (0.0, 0.1)}
    factors = {'L0_ffn_wqkv': 8.0, 'L0_ffn_w1': 8.0, 'L0_ffn_w2': 8.0}
    for name, (base, spread) in spreads.items():
        noise = np.random.default_rng([zlib.crc32(name.encode()), seed]).standard_normal(out[name].shape)
        drawn = base * np.exp(spread * noise) if base else spread * noise
        out[name] = jnp.asarray(drawn.astype(out[name].dtype))
    for name, factor in factors.items():
        out[name] = (out[name] * factor).astype(out[name].dtype)
    return out
```

```python
from contextlib import ExitStack

import concourse.bass as bass
from concourse import mybir

ALU = mybir.AluOpType
ACT = mybir.ActivationFunctionType
AX = mybir.AxisListType
F32 = mybir.dt.float32
F32R = mybir.dt.float32r
F16 = mybir.dt.float16

P = 128
B, S, D = 2, 1024, 128
H, HD = 16, 64
E, F = 8, 352
T = B * S // P
TB = S // P
PAIRS = B * H // 2
VW = 2 * HD + 1
EPS = 1e-5
SCALE = HD ** -0.5
EXP_BIAS = 4.0
V_TOP = 32768.0
POOL_COLS = 832

CH = 8
PCH = 2 * CH
LEAD_S = 2
LEAD_M = 13
PRO_MISC = 9
MISC = 10
F_CHUNKS = [(0, 128), (128, 128), (256, 96)]


def load_and_values(nc, io, mem):
    with ExitStack() as ctx:
        sb = lambda name, shape, dt: ctx.enter_context(nc.sbuf_tensor(name, shape, dt))
        sem = lambda name: ctx.enter_context(nc.semaphore(name))
        xT = sb("xT", [P, T * P], F32)
        wv = sb("wv", [P, H * HD], F32)
        bo = sb("bo", [P, D], F32)
        tops = sb("tops", [P, 2], F32)
        alltops = sb("alltops", [P, 2], F32)
        bound = sb("bound", [P, 2], F32)
        vt = sb("vt", [P, 2, H, VW], F16)
        vps = ctx.enter_context(nc.psum_tensor("vps", [P, 2, 2, 512], F32))
        s_x, s_xT, s_wv, s_bo = sem("s_x"), sem("s_xT"), sem("s_wv"), sem("s_bo")
        s_top, s_alltop, s_bound = sem("s_top"), sem("s_alltop"), sem("s_bound")
        s_zero, s_ident = sem("s_zero"), sem("s_ident")
        s_ones = sem("s_ones")
        s_vps, s_vhi, s_vlo = sem("s_vps"), sem("s_vhi"), sem("s_vlo")
        s_vout = [sem("s_vout0"), sem("s_vout1")]
        block = ctx.enter_context(nc.Block())

        @block.sync
        def _(sp):
            sp.dma_start(xT[:], io["xT"]).then_inc(s_xT, 16)
            sp.dma_start(wv[:], io["Wv"]).then_inc(s_wv, 16)
            sp.dma_start(mem["y"][:], io["x"].rearrange("b (t p) d -> p (b t) d", p=P)).then_inc(s_x, 16)
            sp.dma_start(bo[:], io["bo"].rearrange("(a d) -> a d", a=1).broadcast_to([P, D])).then_inc(s_bo, 16)
            for t in range(T):
                sp.wait_ge(s_vhi, 2 * t + 2)
                sp.wait_ge(s_vlo, 2 * t + 2)
                b, i = divmod(t, TB)
                dst = io["v_dram"][b * H // 2:(b + 1) * H // 2, :, i, :].rearrange("j p c -> p j c")
                sp.dma_start(dst, vt[:, t % 2].rearrange("p (j a) c -> p j (a c)", a=2)).then_inc(s_vout[t % 2], 16)
            for k in range(2):
                sp.wait_ge(s_vout[k], 16 * T // 2)

        @block.gpsimd
        def _(pool):
            nc.gpsimd.memset(mem["ident"][:], 0.0).then_inc(s_zero, 1)
            pool.wait_ge(s_zero, 1)
            nc.gpsimd.affine_select(out=mem["ident"][:], in_=mem["ident"][:], compare_op=ALU.not_equal, fill=1.0,
                                    base=0, pattern=[[-1, P]], channel_multiplier=1).then_inc(s_ident, 1)
            pool.wait_ge(s_top, 2)
            nc.gpsimd.partition_all_reduce(alltops[:], tops[:], P, bass.bass_isa.ReduceOp.max).then_inc(s_alltop, 1)
            pool.wait_ge(s_ident, 1)

        @block.vector
        def _(dve):
            nc.vector.memset(vt[:, :, :, HD:HD + 1], 1.0).then_inc(s_ones, 1)
            dve.wait_ge(s_xT, 16)
            nc.vector.tensor_reduce(tops[:, 0:1], xT[:], AX.X, ALU.max, apply_absolute_value=True).then_inc(s_top, 1)
            dve.wait_ge(s_wv, 16)
            nc.vector.tensor_reduce(tops[:, 1:2], wv[:], AX.X, ALU.max, apply_absolute_value=True).then_inc(s_top, 1)
            dve.wait_ge(s_alltop, 1)
            nc.vector.scalar_tensor_tensor(out=bound[:, 0:1], in0=alltops[:, 0:1], scalar=D / V_TOP,
                                           in1=alltops[:, 1:2], op0=ALU.mult, op1=ALU.mult).then_inc(s_bound, 1)
            dve.wait_ge(s_bound, 1)
            nc.vector.tensor_scalar(mem["vinv"][:], bound[:, 0:1], 1e-30, None, ALU.max).then_inc(s_bound, 1)
            dve.wait_ge(s_bound, 2)
            nc.vector.reciprocal(mem["vscale"][:], mem["vinv"][:]).then_inc(s_bound, 1)
            dve.wait_ge(s_x, 16)
            dve.wait_ge(s_bo, 16)
            nc.vector.tensor_tensor(mem["y"][:], mem["y"][:], bo[:].unsqueeze(1).broadcast_to([P, T, D]), ALU.add)
            dve.wait_ge(s_bound, 3)
            for t in range(T):
                for h in range(2):
                    dve.wait_ge(s_vhi, 2 * t + h + 1)
                    part = vt[:, t % 2, h * H // 2:(h + 1) * H // 2, :]
                    nc.vector.scalar_tensor_tensor(
                        out=part[:, :, HD + 1:VW], in0=vps[:, t % 2, h, :].rearrange("p (h c) -> p h c", c=HD),
                        scalar=mem["vscale"][:, 0:1], in1=part[:, :, 0:HD],
                        op0=ALU.mult, op1=ALU.subtract).then_inc(s_vlo, 1)
            dve.wait_ge(s_ones, 1)

        @block.scalar
        def _(act):
            act.wait_ge(s_bound, 3)
            act.wait_ge(s_ones, 1)
            for t in range(T):
                if t >= 2:
                    act.wait_ge(s_vout[t % 2], 16 * (t // 2))
                for h in range(2):
                    act.wait_ge(s_vps, 2 * t + h + 1)
                    part = vt[:, t % 2, h * H // 2:(h + 1) * H // 2, :]
                    nc.scalar.activation(part[:, :, 0:HD], vps[:, t % 2, h, :].rearrange("p (h c) -> p h c", c=HD),
                                         ACT.Copy, scale=mem["vscale"][:, 0:1]).then_inc(s_vhi, 1)

        @block.tensor
        def _(pe):
            pe.wait_ge(s_xT, 16)
            pe.wait_ge(s_wv, 16)
            for t in range(T):
                for h in range(2):
                    if t >= 2:
                        pe.wait_ge(s_vlo, 2 * (t - 2) + h + 1)
                    nc.tensor.matmul(vps[:, t % 2, h, :], xT[:, t * P:(t + 1) * P], wv[:, h * 512:(h + 1) * 512],
                                     start=True, stop=True).then_inc(s_vps, 1)


def attention(nc, io, mem):
    with ExitStack() as ctx:
        sb = lambda name, shape, dt: ctx.enter_context(nc.sbuf_tensor(name, shape, dt))
        sem = lambda name: ctx.enter_context(nc.semaphore(name))
        wqk = sb("wqk", [P, 2, P], F32)
        xTb = sb("xTb", [P, S], F32)
        hi = sb("hi", [P, 2, S], F32R)
        lo = sb("lo", [P, 2, S], F32R)
        q_hh = sb("q_hh", [P, 2, 2, S], F32R)
        q_lm = sb("q_lm", [P, 2, 2, S], F32R)
        k_hl = sb("k_hl", [P, 2, 2, S], F32R)
        k_h1 = sb("k_h1", [P, 2, 2, S], F32R)
        vbuf = sb("vbuf", [P, 2, TB, 2, VW], F16)
        mx = sb("mx", [P, 2, TB], F32)
        negm = sb("negm", [TB, 2, P], F32R)
        p32 = sb("p32", [P, 2, 1024], F32)
        ph = sb("ph", [P, 4, 1024], F16)
        pl = sb("pl", [P, 4, 1024], F16)
        rec = sb("rec", [P, 2, 4], F32)
        aoT = sb("aoT", [P, 4, P], F32)
        sps = ctx.enter_context(nc.psum_tensor("sps", [P, 2, 1024], F32))
        mps = ctx.enter_context(nc.psum_tensor("mps", [P, 1024], F32))
        ops = ctx.enter_context(nc.psum_tensor("ops", [P, 512], F32))
        misc = ctx.enter_context(nc.psum_tensor("misc", [P, 512], F32))
        O = ops[:, 0:4 * (HD + 1)].rearrange("p (q c) -> p q c", c=HD + 1)

        s_w, s_v, s_wo, s_negm = sem("s_w"), sem("s_v"), sem("s_wo"), sem("s_negm")
        s_head = [sem("s_head0"), sem("s_head1")]
        s_scores, s_maxmm, s_misc, s_pv = sem("s_scores"), sem("s_maxmm"), sem("s_misc"), sem("s_pv")
        s_exp, s_hi = sem("s_exp"), sem("s_hi")
        s_mx, s_subv, s_used, s_oevac = sem("s_mx"), sem("s_subv"), sem("s_used"), sem("s_oevac")
        s_rec, s_init, s_subp = sem("s_rec"), sem("s_init"), sem("s_subp")
        block = ctx.enter_context(nc.Block())

        @block.sync
        def _(sp):
            def ready(x):
                return sp.snap(sp.to_reg(x))

            def load_projection(pair_of_batch, token):
                column = pair_of_batch * P
                sp.dma_start(wqk[:, 0, :], io["Wq"][:, bass.ds(column, P)]).then_inc(s_w, 16)
                sp.dma_start(wqk[:, 1, :], io["Wk"][:, bass.ds(column, P)]).then_inc(s_w, 16)
                sp.dma_start(xTb[:], io["xT"][:, bass.ds(token, S)]).then_inc(s_w, 16)

            def load_values(pair, par):
                sp.dma_start(vbuf[:, par], io["v_dram"][bass.ds(pair, 1), :, :, :].rearrange(
                    "o p t (a c) -> p (o t) a c", a=2)).then_inc(s_v, 16)

            def spread_head(par, a):
                r = slice(HD * a, HD * a + HD)
                for dst, src in ((q_hh[0:HD, par, a, :], hi[r, 0, :]), (q_hh[HD:P, par, a, :], hi[r, 0, :]),
                                 (q_lm[0:HD, par, a, :], lo[r, 0, :]), (k_hl[0:HD, par, a, :], hi[r, 1, :]),
                                 (k_hl[HD:P, par, a, :], lo[r, 1, :]), (k_h1[0:HD, par, a, :], hi[r, 1, :])):
                    sp.dma_start(dst.bitcast(F32), src.bitcast(F32)).then_inc(s_head[a], 16)

            def send_max(par, a):
                sp.dma_start(q_lm[HD:HD + 1, par, a, :].bitcast(F32),
                             negm[:, a, :].bitcast(F32)).then_inc(s_negm, 16)

            sp.dma_start(mem["wo"][:, 1, :], io["Wo"][0:P, :]).then_inc(s_wo, 16)
            load_projection(0, 0)
            load_values(0, 0)
            sp.wait_ge(s_used, 4)
            spread_head(0, 0)
            spread_head(0, 1)
            load_projection(1, 0)
            sp.wait_ge(s_used, 8)
            for a in range(2):
                sp.wait_ge(s_head[a], 96)
                spread_head(1, a)
            sp.wait_ge(s_used, PRO_MISC)
            send_max(0, 0)
            with sp.Fori(0, PAIRS // 2) as it:
                for par in range(2):
                    pp = it * 2 + par
                    next_pair = ready((pp + 1) % PAIRS)
                    wo_row = ready(pp % (H // 2) * P)
                    pair_of_batch = ready((pp + 2) % (H // 2))
                    token = ready((pp + 2) % PAIRS // (H // 2) * S)
                    values_loaded = ready(16 * pp + 16)
                    values_used = ready(PCH * pp + 3)
                    wo_loaded = ready(16 * pp + 16)
                    wo_used = ready(MISC * pp + 4)
                    projected = ready(MISC * pp + 8)
                    maxima_sent = [ready(32 * pp + 16), ready(32 * pp + 32)]
                    jobs = PRO_MISC + MISC * pp
                    maxima_negated = [ready(jobs + 3), ready(jobs + MISC)]
                    pair_split = ready(jobs + 9)
                    head_scored = [ready(PCH * pp + CH), ready(PCH * pp + PCH)]
                    head_spread = ready(96 * pp + 192)
                    sp.wait_ge(s_v, values_loaded)
                    sp.wait_ge(s_scores, values_used)
                    load_values(next_pair, 1 - par)
                    sp.wait_ge(s_misc, wo_used)
                    sp.wait_ge(s_wo, wo_loaded)
                    sp.dma_start(mem["wo"][:, par, :], io["Wo"][bass.ds(wo_row, P), :]).then_inc(s_wo, 16)
                    sp.wait_ge(s_misc, projected)
                    load_projection(pair_of_batch, token)
                    sp.wait_ge(s_negm, maxima_sent[0])
                    sp.wait_ge(s_used, maxima_negated[0])
                    send_max(par, 1)
                    sp.wait_ge(s_used, pair_split)
                    sp.wait_ge(s_scores, head_scored[0])
                    sp.wait_ge(s_head[0], head_spread)
                    spread_head(par, 0)
                    sp.wait_ge(s_negm, maxima_sent[1])
                    sp.wait_ge(s_used, maxima_negated[1])
                    send_max(1 - par, 0)
                    sp.wait_ge(s_scores, head_scored[1])
                    sp.wait_ge(s_head[1], head_spread)
                    spread_head(par, 1)
            for a in range(2):
                sp.wait_ge(s_head[a], 96 * (PAIRS + 2))
            sp.wait_ge(s_v, 16 * (PAIRS + 1))
            sp.wait_ge(s_w, 48 * (PAIRS + 2))
            sp.wait_ge(s_negm, 16 * (2 * PAIRS + 1))
            sp.wait_ge(s_wo, 16 * PAIRS + 16)

        @block.tensor
        def _(pe):
            def scores(par, a, c, n, first_of_head):
                half, kk = divmod(c, CH // 2)
                q = slice(half * 512, half * 512 + 512)
                if first_of_head is not None:
                    pair, head = first_of_head
                    pe.wait_ge(s_head[a], 96 * pair + 96)
                    pe.wait_ge(s_negm, 16 * head + 16)
                buf = c % 2
                if n is not None:
                    pe.wait_ge(s_exp, n - 1)
                for kt in range(2):
                    k = slice((2 * kk + kt) * P, (2 * kk + kt + 1) * P)
                    out = sps[:, buf, kt * 512:(kt + 1) * 512]
                    nc.tensor.matmul(out, k_hl[:, par, a, k], q_hh[:, par, a, q], start=True, stop=False)
                    mm = nc.tensor.matmul(out, k_h1[0:HD + 1, par, a, k], q_lm[0:HD + 1, par, a, q],
                                          start=False, stop=True)
                mm.then_inc(s_scores, 1)

            def maxima(par, a, qt, item, pair=None):
                if pair is not None:
                    pe.wait_ge(s_head[a], 96 * pair + 96)
                if item is not None:
                    pe.wait_ge(s_mx, item)
                for kh in range(2):
                    mm = nc.tensor.matmul(mps[:, kh * 512:(kh + 1) * 512], q_hh[:, par, a, qt * P:(qt + 1) * P],
                                          k_hl[:, par, a, kh * 512:(kh + 1) * 512], start=True, stop=True)
                mm.then_inc(s_maxmm, 1)

            def project(k, job, loads):
                if k == 0:
                    pe.wait_ge(s_w, loads)
                pe.wait_ge(s_used, job)
                nc.tensor.matmul(misc[:], wqk[:, k // 2, :], xTb[:, k % 2 * 512:(k % 2 + 1) * 512],
                                 start=True, stop=True).then_inc(s_misc, 1)

            def turn_maxima(a, job, items):
                pe.wait_ge(s_mx, items)
                pe.wait_ge(s_used, job)
                nc.tensor.transpose(misc[0:TB, 0:P], mx[:, a, :], mem["ident"][:]).then_inc(s_misc, 1)

            def turn_output(par, half, job, units):
                pe.wait_ge(s_oevac, units)
                pe.wait_ge(s_used, job)
                for q in range(4):
                    mm = nc.tensor.transpose(misc[:, q * P:(q + 1) * P], mem["ao"][:, par, 4 * half + q, :],
                                             mem["ident"][:])
                mm.then_inc(s_misc, 1)

            def project_output(par, job, loads):
                pe.wait_ge(s_wo, loads)
                pe.wait_ge(s_used, job)
                for q in range(4):
                    mm = nc.tensor.matmul(misc[:, q * P:(q + 1) * P], aoT[:, q, :], mem["wo"][:, par, :],
                                          start=True, stop=True)
                mm.then_inc(s_misc, 1)

            def values(par, a, c, n, pair):
                half, kk = divmod(c, CH // 2)
                if a == 0 and c == 0:
                    pe.wait_ge(s_v, 16 * pair + 16)
                pe.wait_ge(s_subv, n + 1)
                pe.wait_ge(s_subp, n + 1)
                if kk == 0:
                    pe.wait_ge(s_oevac, 4 * pair + 2 * a + half + 1)
                buf = c % 4
                for kt in range(2):
                    v = vbuf[:, par, 2 * kk + kt, a, :]
                    for q in range(4):
                        w = slice(kt * 512 + q * P, kt * 512 + (q + 1) * P)
                        nc.tensor.matmul(O[:, q, :], ph[:, buf, w], v[:, 0:HD + 1],
                                         start=(kk == 0 and kt == 0 and q == 0), stop=False, skip_group_check=True)
                        nc.tensor.matmul(O[:, q, 0:HD], ph[:, buf, w], v[:, HD + 1:VW],
                                         start=False, stop=False, skip_group_check=True)
                        mm = nc.tensor.matmul(O[:, q, :], pl[:, buf, w], v[:, 0:HD + 1], start=False,
                                              stop=(kk == CH // 2 - 1 and kt == 1 and q == 3), skip_group_check=True)
                mm.then_inc(s_pv, 1)

            for pair in range(2):
                for k in range(4):
                    project(k, 4 * pair + k, 48 * pair + 48)
            for item in range(LEAD_M):
                a, qt = divmod(item, TB)
                maxima(0, a, qt, item, 0 if qt == 0 else None)
                if item == TB:
                    turn_maxima(0, PRO_MISC - 1, TB)
            pe.wait_ge(s_init, 1)
            scores(0, 0, 0, None, (0, 0))
            scores(0, 0, 1, None, None)

            with pe.Fori(0, PAIRS // 2) as it:
                for par in range(2):
                    pp = it * 2 + par
                    job = PRO_MISC + MISC * pp
                    for s in range(PCH):
                        n = PCH * pp + s
                        over, t = divmod(s + LEAD_S, PCH)
                        sa, sc = divmod(t, CH)
                        scores((par + over) % 2, sa, sc, n + LEAD_S,
                               (pp + over, 2 * (pp + over) + sa) if sc == 0 else None)
                        over, t = divmod(s + LEAD_M, PCH)
                        ma, qt = divmod(t, TB)
                        maxima((par + over) % 2, ma, qt, n + LEAD_M, pp + over if qt == 0 else None)
                        if s == 1:
                            turn_output(1 - par, 0, job, 4 * pp + 1)
                        if s == 2:
                            project_output(1 - par, job + 1, 16 * pp + 16)
                        if s == 3:
                            turn_maxima(1, job + 2, PCH * pp + 16)
                        if s == 4:
                            turn_output(1 - par, 1, job + 3, 4 * pp + 1)
                        if s == 5:
                            project_output(1 - par, job + 4, 16 * pp + 16)
                        if 7 <= s < 11:
                            project(s - 7, job + 5 + s - 7, 48 * pp + 144)
                        if s == 11:
                            turn_maxima(0, job + 9, PCH * pp + 24)
                        values(par, s // CH, s % CH, n, pp)
            job = PRO_MISC + MISC * PAIRS
            for half in range(2):
                turn_output(1, half, job + 2 * half, 4 * PAIRS + 1)
                project_output(1, job + 2 * half + 1, 16 * PAIRS + 16)

        @block.scalar
        def _(act):
            def exps(c, n):
                act.wait_ge(s_scores, n + 1)
                if c is not None:
                    act.wait_ge(s_subv, n - 1)
                    act.wait_ge(s_subp, n - 1)
                buf = n % 2 if c is None else c
                q = n if c is None else c
                nc.scalar.activation(p32[:, buf % 2, :], sps[:, buf % 2, :], ACT.Exp, bias=EXP_BIAS, scale=SCALE)
                nc.scalar.activation(ph[:, q % 4, :], sps[:, buf % 2, :], ACT.Exp, bias=EXP_BIAS, scale=SCALE).then_inc(s_exp, 1)

            def round_piece(k, job, spread):
                if spread is not None and k == 0:
                    for a in range(2):
                        act.wait_ge(s_head[a], spread)
                act.wait_ge(s_misc, job + 1)
                nc.scalar.copy(hi[:, k // 2, k % 2 * 512:(k % 2 + 1) * 512], misc[:]).then_inc(s_hi, 1)

            for pair in range(2):
                for k in range(4):
                    round_piece(k, 4 * pair + k, 96 * pair if pair else None)
            exps(None, 0)
            exps(None, 1)
            with act.Fori(0, PAIRS // 2) as it:
                for par in range(2):
                    pp = it * 2 + par
                    for s in range(PCH):
                        exps((s + LEAD_S) % CH, PCH * pp + s + LEAD_S)
                        if 7 <= s < 11:
                            k = s - 7
                            round_piece(k, PRO_MISC + MISC * pp + 5 + k, 96 * pp + 192)

        @block.gpsimd
        def _(pool):
            def low_parts(c, n):
                pool.wait_ge(s_exp, n + 1)
                nc.gpsimd.tensor_tensor(pl[:, c % 4, 0:POOL_COLS], p32[:, c % 2, 0:POOL_COLS],
                                        ph[:, c % 4, 0:POOL_COLS], ALU.subtract).then_inc(s_subp, 1)

            low_parts(0, 0)
            low_parts(1, 1)
            with pool.Fori(0, PAIRS * PCH // 4) as it:
                for s in range(4):
                    low_parts(s + LEAD_S, it * 4 + s + LEAD_S)

        @block.vector
        def _(dve):
            def reduce_max(slot, qt, item):
                dve.wait_ge(s_maxmm, item + 1)
                nc.vector.tensor_reduce(mx[:, slot, qt:qt + 1], mps[:], AX.X, ALU.max).then_inc(s_mx, 1)

            def low_parts(c, n):
                dve.wait_ge(s_exp, n + 1)
                nc.vector.tensor_tensor(pl[:, c % 4, POOL_COLS:], p32[:, c % 2, POOL_COLS:],
                                        ph[:, c % 4, POOL_COLS:], ALU.subtract).then_inc(s_subv, 1)

            def rest_of_piece(k, job, pieces):
                dve.wait_ge(s_hi, pieces)
                cols = slice(k % 2 * 512, (k % 2 + 1) * 512)
                nc.vector.tensor_tensor(lo[:, k // 2, cols], misc[:], hi[:, k // 2, cols],
                                        ALU.subtract).then_inc(s_used, 1)

            def negate_maxima(a, job, sent):
                if sent is not None:
                    dve.wait_ge(s_negm, sent)
                dve.wait_ge(s_misc, job + 1)
                nc.vector.tensor_scalar(negm[:, a, :], misc[0:TB, 0:P], -1.0, None, ALU.mult).then_inc(s_used, 1)

            def take_turned(job):
                dve.wait_ge(s_misc, job + 1)
                nc.vector.tensor_copy(aoT[:].rearrange("p q t -> p (q t)"), misc[:]).then_inc(s_used, 1)

            def add_output(batch, half, job):
                dve.wait_ge(s_misc, job + 1)
                y = mem["y"][:, bass.ds(batch * TB + 4 * half, 4), :]
                nc.vector.tensor_tensor(y, misc[:].rearrange("p (q d) -> p q d", q=4), y, ALU.add).then_inc(s_used, 1)

            def normalise(par, a, half, unit):
                dve.wait_ge(s_pv, 4 * unit + 4)
                nc.vector.reciprocal(rec[:, 0, :], O[:, :, HD]).then_inc(s_rec, 1)
                dve.wait_ge(s_rec, 2 * unit + 1)
                nc.vector.tensor_scalar(rec[:, 1, :], rec[:, 0, :], mem["vinv"][:, 0:1], None,
                                        ALU.mult).then_inc(s_rec, 1)
                dve.wait_ge(s_rec, 2 * unit + 2)
                nc.vector.tensor_tensor(mem["ao"][:, par, 4 * half:4 * half + 4, a * HD:(a + 1) * HD], O[:, :, 0:HD],
                                        rec[:, 1, :].unsqueeze(2).broadcast_to([P, 4, HD]),
                                        ALU.mult).then_inc(s_oevac, 1)

            nc.vector.memset(k_h1[HD:HD + 1].bitcast(F32), 1.0).then_inc(s_init, 1)
            nc.vector.memset(mem["ao"][:, 1], 0.0).then_inc(s_oevac, 1)
            for pair in range(2):
                for k in range(4):
                    rest_of_piece(k, 4 * pair + k, 4 * pair + k + 1)
            for item in range(LEAD_M):
                reduce_max(item // TB, item % TB, item)
                if item == TB:
                    negate_maxima(0, PRO_MISC - 1, None)
            low_parts(0, 0)
            with dve.Fori(0, PAIRS // 2) as it:
                for par in range(2):
                    pp = it * 2 + par
                    job = PRO_MISC + MISC * pp
                    for s in range(PCH):
                        n = PCH * pp + s
                        ma, qt = divmod((s + LEAD_M) % PCH, TB)
                        reduce_max(ma, qt, n + LEAD_M)
                        if s in (4, 8, 12):
                            u = s // 4 - 1
                            normalise(par, u // 2, u % 2, 4 * pp + u)
                        before = (pp + PAIRS - 1) % PAIRS // (H // 2)
                        if s in (1, 4):
                            take_turned(job + s - 1)
                        if s in (2, 5):
                            add_output(before, s // 4, job + s - 1)
                        if s == 3:
                            negate_maxima(1, job + 2, 32 * pp + 16)
                        if 7 <= s < 11:
                            rest_of_piece(s - 7, job + 5 + s - 7, 4 * pp + 9 + s - 7)
                        if s == 11:
                            negate_maxima(0, job + 9, 32 * pp + 16)
                        low_parts((s + 1) % CH, n + 1)
                    normalise(par, 1, 1, 4 * pp + 3)
            job = PRO_MISC + MISC * PAIRS
            for half in range(2):
                take_turned(job + 2 * half)
                add_output(B - 1, half, job + 2 * half + 1)


def norm_and_gates(nc, io, mem):
    with ExitStack() as ctx:
        sb = lambda name, shape, dt: ctx.enter_context(nc.sbuf_tensor(name, shape, dt))
        sem = lambda name: ctx.enter_context(nc.semaphore(name))
        sq = sb("sq", [P, T, D], F32)
        st = sb("st", [P, 6, T], F32)
        wg = sb("wg", [P, 3 * E], F32)
        mixed = sb("mixed", [P, T, 3 * E], F32)
        prod = sb("prod", [P, T, E, E], F32)
        pv = sb("pv", [P, T, E, E], F32)
        g = sb("g", [P, 12, T, E], F32)
        one = sb("one", [P, 8, T], F32)
        rank = sb("rank", [P, E], F32)
        tps = ctx.enter_context(nc.psum_tensor("tps", [P, 2, 512], F32))
        gps = ctx.enter_context(nc.psum_tensor("gps", [P, 512], F32))
        s_wg, s_chain, s_sq, s_root = sem("s_wg"), sem("s_chain"), sem("s_sq"), sem("s_root")
        s_x1, s_turn, s_copied, s_mixed = sem("s_x1"), sem("s_turn"), sem("s_copied"), sem("s_mixed")
        s_shift, s_exp = sem("s_shift"), sem("s_exp")
        block = ctx.enter_context(nc.Block())

        @block.sync
        def _(sp):
            sp.dma_start(wg[:], io["wqkvT"]).then_inc(s_wg, 16)
            sp.wait_ge(s_wg, 16)

        @block.tensor
        def _(pe):
            pe.wait_ge(s_x1, 1)
            for t in range(T):
                if t >= 8 and t % 4 == 0:
                    pe.wait_ge(s_copied, t // 4 - 1)
                tr = nc.tensor.transpose(tps[:, t // 4 % 2, t % 4 * P:(t % 4 + 1) * P], mem["y"][:, t, :],
                                         mem["ident"][:])
                if t % 4 == 3:
                    tr.then_inc(s_turn, 1)
            pe.wait_ge(s_wg, 16)
            for t in range(T):
                if t % 4 == 0:
                    pe.wait_ge(s_copied, t // 4 + 1)
                mm = nc.tensor.matmul(gps[:, t * 3 * E:(t + 1) * 3 * E], mem["x1T"][:, t * P:(t + 1) * P], wg[:],
                                      start=True, stop=True)
            mm.then_inc(s_mixed, 1)

        @block.scalar
        def _(act):
            layer_norm_act(nc, act, mem["y"], sq, st, s_chain, s_sq, s_root)
            for k in range(T // 4):
                act.wait_ge(s_turn, k + 1)
                nc.scalar.copy(mem["x1T"][:, k * 512:(k + 1) * 512], tps[:, k % 2, :]).then_inc(s_copied, 1)
            act.wait_ge(s_shift, 1)
            nc.scalar.activation(prod[:], prod[:], ACT.Exp).then_inc(s_exp, 1)
            act.wait_ge(s_shift, 2)
            nc.scalar.activation(one[:, 2, :], one[:, 1, :], ACT.Exp).then_inc(s_exp, 1)

        @block.vector
        def _(dve):
            steps = [0]

            def then(ins):
                steps[0] += 1
                ins.then_inc(s_chain, 1)
                dve.wait_ge(s_chain, steps[0])

            layer_norm_dve(nc, dve, then, mem["y"], mem["y"], sq, st, s_sq, s_root, s_x1)
            for e in range(E):
                last = nc.vector.memset(rank[:, e:e + 1], float(E - e))
            then(last)
            dve.wait_ge(s_mixed, 1)
            then(nc.vector.tensor_copy(mixed[:].rearrange("p t c -> p (t c)"), gps[:, 0:T * 3 * E]))
            q, k, v = (mixed[:, :, i * E:(i + 1) * E] for i in range(3))
            full = [P, T, E, E]
            rows = lambda x: x.unsqueeze(3).broadcast_to(full)
            cols = lambda x: x.unsqueeze(2).broadcast_to(full)
            then(nc.vector.tensor_tensor(prod[:], rows(q), cols(k), ALU.mult))
            then(nc.vector.tensor_reduce(g[:, 0], prod[:], AX.X, ALU.max))
            nc.vector.tensor_tensor(prod[:], prod[:], rows(g[:, 0]), ALU.subtract).then_inc(s_shift, 1)
            dve.wait_ge(s_exp, 1)
            then(nc.vector.tensor_reduce(g[:, 1], prod[:], AX.X, ALU.add))
            then(nc.vector.tensor_tensor(pv[:], prod[:], cols(v), ALU.mult))
            then(nc.vector.tensor_reduce(g[:, 2], pv[:], AX.X, ALU.add))
            then(nc.vector.reciprocal(g[:, 3], g[:, 1]))
            then(nc.vector.tensor_tensor(g[:, 4], g[:, 2], g[:, 3], ALU.mult))
            each = lambda x: x.unsqueeze(2).broadcast_to([P, T, E])
            ranks = rank[:].unsqueeze(1).broadcast_to([P, T, E])

            def largest(logits, top, first, hot, scratch):
                then(nc.vector.tensor_reduce(top, logits, AX.X, ALU.max))
                then(nc.vector.tensor_tensor(scratch, logits, each(top), ALU.is_equal))
                then(nc.vector.tensor_tensor(scratch, scratch, ranks, ALU.mult))
                then(nc.vector.tensor_reduce(first, scratch, AX.X, ALU.max))
                then(nc.vector.tensor_tensor(hot, ranks, each(first), ALU.is_equal))

            largest(g[:, 4], one[:, 4, :], one[:, 5, :], g[:, 5], g[:, 6])
            then(nc.vector.scalar_tensor_tensor(out=g[:, 7], in0=g[:, 5], scalar=-3e38, in1=g[:, 4],
                                                op0=ALU.mult, op1=ALU.add))
            largest(g[:, 7], one[:, 6, :], one[:, 7, :], g[:, 8], g[:, 6])
            nc.vector.tensor_tensor(one[:, 1, :], one[:, 6, :], one[:, 4, :], ALU.subtract).then_inc(s_shift, 1)
            dve.wait_ge(s_exp, 2)
            then(nc.vector.tensor_scalar(one[:, 3, :], one[:, 2, :], 1.0, None, ALU.add))
            then(nc.vector.reciprocal(one[:, 0, :], one[:, 3, :]))
            then(nc.vector.tensor_tensor(one[:, 5, :], one[:, 2, :], one[:, 0, :], ALU.mult))
            then(nc.vector.tensor_tensor(g[:, 9], g[:, 5], each(one[:, 0, :]), ALU.mult))
            then(nc.vector.tensor_tensor(g[:, 10], g[:, 8], each(one[:, 5, :]), ALU.mult))
            then(nc.vector.tensor_tensor(mem["gate"][:], g[:, 9], g[:, 10], ALU.add))


def layer_norm_act(nc, act, src, sq, st, s_chain, s_sq, s_root):
    act.wait_ge(s_chain, 3)
    nc.scalar.activation(sq[:], src[:], ACT.Square).then_inc(s_sq, 1)
    act.wait_ge(s_chain, 5)
    nc.scalar.activation(st[:, 4, :], st[:, 3, :], ACT.Sqrt).then_inc(s_root, 1)


def layer_norm_dve(nc, dve, then, src, dst, sq, st, s_sq, s_root, s_done):
    full = [P, T, D]
    each = lambda x: x.unsqueeze(2).broadcast_to(full)
    then(nc.vector.tensor_reduce(st[:, 0, :], src[:], AX.X, ALU.add))
    then(nc.vector.tensor_scalar(st[:, 1, :], st[:, 0, :], 1.0 / D, None, ALU.mult))
    then(nc.vector.tensor_tensor(src[:], src[:], each(st[:, 1, :]), ALU.subtract))
    dve.wait_ge(s_sq, 1)
    then(nc.vector.tensor_reduce(st[:, 2, :], sq[:], AX.X, ALU.add))
    then(nc.vector.tensor_scalar(st[:, 3, :], st[:, 2, :], 1.0 / D, EPS, ALU.mult, ALU.add))
    dve.wait_ge(s_root, 1)
    then(nc.vector.reciprocal(st[:, 5, :], st[:, 4, :]))
    nc.vector.tensor_tensor(dst[:], src[:], each(st[:, 5, :]), ALU.mult).then_inc(s_done, 1)


def experts(nc, io, mem):
    BL = T // 4
    NC = len(F_CHUNKS)
    UNITS = BL * 2
    with ExitStack() as ctx:
        sb = lambda name, shape, dt: ctx.enter_context(nc.sbuf_tensor(name, shape, dt))
        sem = lambda name: ctx.enter_context(nc.semaphore(name))
        w1 = sb("w1", [P, 2, 2 * F], F32)
        w2 = sb("w2", [P, 2, NC, D], F32)
        silu = sb("silu", [P, 2, 512], F32)
        he = sb("he", [P, 2, 512], F32)
        part = sb("part", [P, 4, D], F32)
        aps = ctx.enter_context(nc.psum_tensor("aps", [P, 2, 512], F32))
        gps = ctx.enter_context(nc.psum_tensor("gps2", [P, 2, 512], F32))
        yps = ctx.enter_context(nc.psum_tensor("yps", [P, 2, 512], F32))
        s_w = [sem("s_we0"), sem("s_we1")]
        s_h, s_silu, s_he, s_y, s_part, s_add = (sem(n) for n in ("s_h", "s_silu", "s_he", "s_y", "s_part", "s_add"))
        block = ctx.enter_context(nc.Block())

        @block.sync
        def _(sp):
            def ready(x):
                return sp.snap(sp.to_reg(x))

            def load(e, par):
                sp.dma_start(w1[:, par, :], io["w1T"][bass.ds(e, 1), :, :].rearrange("o h f -> h (o f)"))\
                    .then_inc(s_w[par], 16)
                sp.dma_start(w2[:, par, 0:2, :], io["w2T"][bass.ds(e, 1), 0:2 * P, :].rearrange(
                    "o (c p) h -> p (o c) h", p=P)).then_inc(s_w[par], 16)
                sp.dma_start(w2[0:F - 2 * P, par, 2, :], io["w2T"][bass.ds(e, 1), 2 * P:F, :].rearrange(
                    "o p h -> (o p) h")).then_inc(s_w[par], 16)

            load(0, 0)
            load(1, 1)
            with sp.Fori(0, E // 2 - 1) as it:
                for par in range(2):
                    expert = ready(it * 2 + par + 2)
                    used = ready(it * UNITS + (par + 1) * BL)
                    loaded = ready(it * 48 + 48)
                    sp.wait_ge(s_y, used)
                    sp.wait_ge(s_w[par], loaded)
                    load(expert, par)
            for par in range(2):
                sp.wait_ge(s_w[par], 48 * E // 2)

        @block.tensor
        def _(pe):
            def hidden(par, bl, c, k):
                off, n = F_CHUNKS[c]
                x = mem["x1T"][:, bl * 512:(bl + 1) * 512]
                nc.tensor.matmul(aps[0:n, k % 2, :], w1[:, par, off:off + n], x, start=True, stop=True)
                nc.tensor.matmul(gps[0:n, k % 2, :], w1[:, par, F + off:F + off + n], x,
                                 start=True, stop=True).then_inc(s_h, 1)

            def down(par, u, c, k, kk):
                pe.wait_ge(s_he, kk + 1)
                n = F_CHUNKS[c][1]
                for q in range(4):
                    mm = nc.tensor.matmul(yps[:, u % 2, q * D:(q + 1) * D], he[0:n, k % 2, q * P:(q + 1) * P],
                                          w2[0:n, par, c, :], start=(c == 0 and q == 0), stop=(c == NC - 1 and q == 3),
                                          skip_group_check=True)
                if c == NC - 1:
                    mm.then_inc(s_y, 1)

            with pe.Fori(0, E // 2) as it:
                for u in range(UNITS):
                    par, bl = divmod(u, BL)
                    unit = it * UNITS + u
                    if bl == 0:
                        pe.wait_ge(s_w[par], it * 48 + 48)
                    for c in range(NC):
                        k = u * NC + c
                        kk = unit * NC + c
                        if c >= 2:
                            pe.wait_ge(s_he, kk - 1)
                        hidden(par, bl, c, k)
                        if c:
                            down(par, u, c - 1, k - 1, kk - 1)
                    down(par, u, NC - 1, k, kk)

        @block.scalar
        def _(act):
            with act.Fori(0, E // 2) as it:
                for u in range(UNITS):
                    for c in range(NC):
                        k = u * NC + c
                        kk = it * (UNITS * NC) + k
                        n = F_CHUNKS[c][1]
                        act.wait_ge(s_h, kk + 1)
                        nc.scalar.activation(silu[0:n, k % 2, :], aps[0:n, k % 2, :], ACT.Silu).then_inc(s_silu, 1)

        @block.vector
        def _(dve):
            def gated(k, kk, n):
                dve.wait_ge(s_silu, kk + 1)
                nc.vector.tensor_tensor(he[0:n, k % 2, :], silu[0:n, k % 2, :], gps[0:n, k % 2, :],
                                        ALU.mult).then_inc(s_he, 1)

            with dve.Fori(0, E // 2) as it:
                for u in range(UNITS):
                    par, bl = divmod(u, BL)
                    unit = it * UNITS + u
                    for c in range(NC):
                        k = u * NC + c
                        gated(k, unit * NC + c, F_CHUNKS[c][1])
                    dve.wait_ge(s_y, unit + 1)
                    gate = mem["gate"][:, bl * 4:(bl + 1) * 4, bass.ds(it * 2 + par, 1)].broadcast_to([P, 4, D])
                    nc.vector.tensor_tensor(part[:], yps[:, u % 2, :].rearrange("p (q d) -> p q d", q=4), gate,
                                            ALU.mult).then_inc(s_part, 1)
                    dve.wait_ge(s_part, unit + 1)
                    y = mem["acc"][:, bl * 4:(bl + 1) * 4, :]
                    nc.vector.tensor_tensor(y, y, part[:], ALU.add).then_inc(s_add, 1)


def finish(nc, io, mem):
    with ExitStack() as ctx:
        sb = lambda name, shape, dt: ctx.enter_context(nc.sbuf_tensor(name, shape, dt))
        sem = lambda name: ctx.enter_context(nc.semaphore(name))
        sq = sb("sq2", [P, T, D], F32)
        st = sb("st2", [P, 6, T], F32)
        s_chain, s_sq, s_root, s_done, s_out = (sem(n) for n in ("s_chain2", "s_sq2", "s_root2", "s_done", "s_out"))
        block = ctx.enter_context(nc.Block())

        @block.scalar
        def _(act):
            layer_norm_act(nc, act, mem["acc"], sq, st, s_chain, s_sq, s_root)

        @block.vector
        def _(dve):
            steps = [0]

            def then(ins):
                steps[0] += 1
                ins.then_inc(s_chain, 1)
                dve.wait_ge(s_chain, steps[0])

            layer_norm_dve(nc, dve, then, mem["acc"], mem["acc"], sq, st, s_sq, s_root, s_done)

        @block.sync
        def _(sp):
            sp.wait_ge(s_done, 1)
            sp.dma_start(io["out"].rearrange("b (t p) d -> p (b t) d", p=P), mem["acc"][:]).then_inc(s_out, 16)
            sp.wait_ge(s_out, 16)


def bass_transformer_layer_moe(nc, x, xT, Wq, Wk, Wv, Wo, bo, wqkvT, w1T, w2T, out):
    io = dict(x=x, xT=xT, Wq=Wq, Wk=Wk, Wv=Wv, Wo=Wo, bo=bo, wqkvT=wqkvT, w1T=w1T, w2T=w2T, out=out)
    io["v_dram"] = nc.dram_tensor("v_dram", [PAIRS, P, TB, 2 * VW], F16, kind="Internal").ap()
    with ExitStack() as ctx:
        sb = lambda name, shape, dt: ctx.enter_context(nc.sbuf_tensor(name, shape, dt))
        mem = {
            "ident": sb("ident", [P, P], F32),
            "y": sb("y", [P, T, D], F32),
            "ao": sb("ao", [P, 2, TB, P], F32),
            "wo": sb("wo", [P, 2, D], F32),
            "vinv": sb("vinv", [P, 1], F32),
            "vscale": sb("vscale", [P, 1], F32),
        }
        load_and_values(nc, io, mem)
        attention(nc, io, mem)
        mem["x1T"] = sb("x1T", [P, T * P], F32)
        mem["gate"] = sb("gate", [P, T, E], F32)
        norm_and_gates(nc, io, mem)
        mem["acc"] = mem["y"]
        experts(nc, io, mem)
        finish(nc, io, mem)


def kernel(L0_attn_x, L0_attn_Wq, L0_attn_Wk, L0_attn_Wv, L0_attn_Wo, L0_attn_bo, L0_ffn_wqkv, L0_ffn_w1, L0_ffn_w2):
    import numpy as np
    import concourse.bacc as bacc
    from concourse.bass_utils import run_bass_kernel_spmd

    x = np.ascontiguousarray(L0_attn_x)
    ins = {
        "x": x,
        "xT": np.ascontiguousarray(x.reshape(B * S, D).T),
        "Wq": L0_attn_Wq, "Wk": L0_attn_Wk, "Wv": L0_attn_Wv, "Wo": L0_attn_Wo, "bo": L0_attn_bo,
        "wqkvT": np.ascontiguousarray(np.asarray(L0_ffn_wqkv).T),
        "w1T": np.ascontiguousarray(np.asarray(L0_ffn_w1).transpose(0, 2, 1)),
        "w2T": np.ascontiguousarray(np.asarray(L0_ffn_w2).transpose(0, 2, 1)),
    }
    nc = bacc.Bacc("TRN2", target_bir_lowering=False, num_devices=1)
    arrays, args = {}, []
    for name, a in ins.items():
        a = np.ascontiguousarray(a)
        arrays[f"in_{name}"] = a
        args.append(nc.dram_tensor(f"in_{name}", a.shape, mybir.dt.from_np(a.dtype), kind="ExternalInput").ap())
    args.append(nc.dram_tensor("out_0", (B, S, D), F32, kind="ExternalOutput").ap())
    bass_transformer_layer_moe(nc, *args)
    r = run_bass_kernel_spmd(nc, [arrays], core_ids=[0])
    return r.results[0]["out_0"]
```

```python
from contextlib import ExitStack

import concourse.bass as bass
from concourse import mybir

ALU = mybir.AluOpType
ACT = mybir.ActivationFunctionType
AX = mybir.AxisListType
F32 = mybir.dt.float32
F32R = mybir.dt.float32r
F16 = mybir.dt.float16

P = 128
B, S, D = 2, 1024, 128
H, HD = 16, 64
E, F = 8, 352
T = B * S // P
TB = S // P
PAIRS = B * H // 2
VW = 2 * HD + 1
EPS = 1e-5
SCALE = HD ** -0.5
EXP_BIAS = 4.0
V_TOP = 32768.0
POOL_COLS = 896

CH = 8
PCH = 2 * CH
LEAD_S = 3
LEAD_M = 14
PRO_MISC = 9
P1_TILE = 8
V_BUFS = 4
JOBS = {1: ("maxima", 1), 2: ("project", 0), 4: ("project", 1), 5: ("project", 2), 7: ("project", 3),
        9: ("maxima", 0), 10: ("turn", 0), 11: ("add", 0), 12: ("turn", 1), 13: ("add", 1)}
MISC = len(JOBS)
job_of_slot = {slot: k for k, slot in enumerate(JOBS)}
F_CHUNKS = [(0, 128), (128, 128), (256, 96)]


def attention(nc, io, mem):
    with ExitStack() as ctx:
        sb = lambda name, shape, dt: ctx.enter_context(nc.sbuf_tensor(name, shape, dt))
        sem = lambda name: ctx.enter_context(nc.semaphore(name))
        xT = sb("xT", [P, T * P], F32)
        wv = sb("wv", [P, H * HD], F32)
        bo = sb("bo", [P, D], F32)
        tops = sb("tops", [P, 2], F32)
        alltops = sb("alltops", [P, 2], F32)
        bound = sb("bound", [P, 1], F32)
        vinv = sb("vinv", [P, 1], F32)
        vscale = sb("vscale", [P, 1], F32)
        vt = sb("vt", [P, V_BUFS, H, VW], F16)
        wqk = sb("wqk", [P, 2, P], F32)
        wqk_hi = sb("wqk_hi", [P, 2, P], F32R)
        wqk_lo = sb("wqk_lo", [P, 2, P], F32R)
        xT_hi = sb("xT_hi", [P, T * P], F32R)
        xT_lo = sb("xT_lo", [P, T * P], F32R)
        hi = sb("hi", [P, 2, S], F32R)
        lo = sb("lo", [P, 2, S], F32R)
        q_hh = sb("q_hh", [P, 2, 2, S], F32R)
        q_lm = sb("q_lm", [P, 2, 2, S], F32R)
        k_hl = sb("k_hl", [P, 2, 2, S], F32R)
        k_h1 = sb("k_h1", [P, 2, 2, S], F32R)
        vbuf = sb("vbuf", [P, 2, TB, 2, VW], F16)
        mx = sb("mx", [P, 2, TB], F32)
        negm = sb("negm", [TB, 2, P], F32R)
        p32 = sb("p32", [P, 4, 1024], F32)
        ph = sb("ph", [P, 4, 1024], F16)
        pl = sb("pl", [P, 4, 1024], F16)
        rec = sb("rec", [P, 4], F32)
        aoT = sb("aoT", [P, 4, P], F32)
        sps = ctx.enter_context(nc.psum_tensor("sps", [P, 2, 1024], F32))
        mps = ctx.enter_context(nc.psum_tensor("mps", [P, 1024], F32))
        ops = ctx.enter_context(nc.psum_tensor("ops", [P, 512], F32))
        misc = ctx.enter_context(nc.psum_tensor("misc", [P, 512], F32))
        O = ops[:, 0:4 * (HD + 1)].rearrange("p (q c) -> p q c", c=HD + 1)

        p_banks = [misc[:], ops[:], mps[:, 0:512], mps[:, 512:1024]]

        s_x, s_xT, s_wv, s_bo = sem("s_x"), sem("s_xT"), sem("s_wv"), sem("s_bo")
        s_top, s_alltop, s_bound = sem("s_top"), sem("s_alltop"), sem("s_bound")
        s_zero, s_ident, s_ones, s_xbo = sem("s_zero"), sem("s_ident"), sem("s_ones"), sem("s_xbo")
        s_vps, s_vhi, s_vlo = sem("s_vps"), sem("s_vhi"), sem("s_vlo")
        s_vout = [sem(f"s_vout{k}") for k in range(V_BUFS)]
        s_w, s_v, s_wo, s_negm = sem("s_w"), sem("s_v"), sem("s_wo"), sem("s_negm")
        s_head = [sem("s_head0"), sem("s_head1")]
        s_scores, s_maxmm, s_misc, s_pv = sem("s_scores"), sem("s_maxmm"), sem("s_misc"), sem("s_pv")
        s_exp, s_hi = sem("s_exp"), sem("s_hi")
        s_mx, s_subv, s_used, s_oevac = sem("s_mx"), sem("s_subv"), sem("s_used"), sem("s_oevac")
        s_whi, s_wlo, s_xhi, s_xlo = sem("s_whi"), sem("s_wlo"), sem("s_xhi"), sem("s_xlo")
        s_rec, s_init, s_subp = sem("s_rec"), sem("s_init"), sem("s_subp")
        block = ctx.enter_context(nc.Block())

        @block.sync
        def _(sp):
            def ready(x):
                return sp.snap(sp.to_reg(x))

            def load_projection(pair_of_batch):
                column = pair_of_batch * P
                sp.dma_start(wqk[:, 0, :], io["Wq"][:, bass.ds(column, P)]).then_inc(s_w, 16)
                sp.dma_start(wqk[:, 1, :], io["Wk"][:, bass.ds(column, P)]).then_inc(s_w, 16)

            def load_values(row, par):
                sp.dma_start(vbuf[:, par], io["v_dram"][bass.ds(row, 1), :, :, :].rearrange(
                    "o p t (a c) -> p (o t) a c", a=2)).then_inc(s_v, 16)

            def spread_head(par, a):
                r = slice(HD * a, HD * a + HD)
                for dst, src in ((q_hh[0:HD, par, a, :], hi[r, 0, :]), (q_hh[HD:P, par, a, :], hi[r, 0, :]),
                                 (q_lm[0:HD, par, a, :], lo[r, 0, :]), (k_hl[0:HD, par, a, :], hi[r, 1, :]),
                                 (k_hl[HD:P, par, a, :], lo[r, 1, :]), (k_h1[0:HD, par, a, :], hi[r, 1, :])):
                    sp.dma_start(dst.bitcast(F32), src.bitcast(F32)).then_inc(s_head[a], 16)

            load_projection(0)
            sp.dma_start(xT[:], io["xT"]).then_inc(s_xT, 16)
            sp.dma_start(wv[:], io["Wv"]).then_inc(s_wv, 16)
            sp.dma_start(mem["y"][:], io["x"].rearrange("b (t p) d -> p (b t) d", p=P)).then_inc(s_x, 16)
            sp.dma_start(bo[:], io["bo"].rearrange("(a d) -> a d", a=1).broadcast_to([P, D])).then_inc(s_bo, 16)
            sp.dma_start(mem["wo"][:, 1, :], io["Wo"][0:P, :]).then_inc(s_wo, 16)
            sp.wait_ge(s_used, 4)
            spread_head(0, 0)
            spread_head(0, 1)
            for k in range(V_BUFS):
                sp.wait_ge(s_vout[k], 16 * TB // V_BUFS)
            load_values(0, 0)
            sp.wait_ge(s_used, 8)
            load_projection(1)
            for a in range(2):
                sp.wait_ge(s_head[a], 96)
                spread_head(1, a)
            for k in range(V_BUFS):
                sp.wait_ge(s_vout[k], 16 * T // V_BUFS)
            with sp.Fori(0, PAIRS // 2) as it:
                pair_of_batch = ready((it + 2) % (H // 2))
                weights_split = ready(it + 1)
                weights_loaded = ready(32 * it + 64)
                sp.wait_ge(s_wlo, weights_split)
                sp.wait_ge(s_w, weights_loaded)
                load_projection(pair_of_batch)
                for par in range(2):
                    pp = it * 2 + par
                    next_values = ready(it + H // 2) if par == 0 else ready((it + 1) % (H // 2))
                    wo_row = ready(it * P)
                    values_loaded = ready(16 * pp + 16)
                    values_used = ready(PCH * pp + LEAD_S + 1)
                    wo_loaded = ready(16 * pp + 16)
                    wo_used = ready(PRO_MISC + MISC * pp)
                    pair_split = ready(PRO_MISC + MISC * pp + 5)
                    head_scored = [ready(PCH * pp + CH), ready(PCH * pp + PCH)]
                    head_spread = ready(96 * pp + 192)
                    sp.wait_ge(s_v, values_loaded)
                    sp.wait_ge(s_scores, values_used)
                    load_values(next_values, 1 - par)
                    sp.wait_ge(s_misc, wo_used)
                    sp.wait_ge(s_wo, wo_loaded)
                    sp.dma_start(mem["wo"][:, par, :], io["Wo"][bass.ds(wo_row, P), :]).then_inc(s_wo, 16)
                    sp.wait_ge(s_used, pair_split)
                    sp.wait_ge(s_scores, head_scored[0])
                    sp.wait_ge(s_head[0], head_spread)
                    spread_head(par, 0)
                    sp.wait_ge(s_scores, head_scored[1])
                    sp.wait_ge(s_head[1], head_spread)
                    spread_head(par, 1)
            for a in range(2):
                sp.wait_ge(s_head[a], 96 * (PAIRS + 2))
            sp.wait_ge(s_v, 16 * (PAIRS + 1))
            sp.wait_ge(s_w, 32 * (PAIRS // 2 + 2))
            sp.wait_ge(s_wo, 16 * PAIRS + 16)

        @block.tensor
        def _(pe):
            def scores(par, a, c, n, first_of_head):
                half, kk = divmod(c, CH // 2)
                q = slice(half * 512, half * 512 + 512)
                if first_of_head is not None:
                    pair, head = first_of_head
                    pe.wait_ge(s_head[a], 96 * pair + 96)
                    pe.wait_ge(s_negm, 16 * head + 16)
                buf = c % 2
                if n is not None:
                    pe.wait_ge(s_exp, n - 1)
                for kt in range(2):
                    k = slice((2 * kk + kt) * P, (2 * kk + kt + 1) * P)
                    out = sps[:, buf, kt * 512:(kt + 1) * 512]
                    nc.tensor.matmul(out, k_hl[:, par, a, k], q_hh[:, par, a, q], start=True, stop=False)
                    mm = nc.tensor.matmul(out, k_h1[0:HD + 1, par, a, k], q_lm[0:HD + 1, par, a, q],
                                          start=False, stop=True)
                mm.then_inc(s_scores, 1)

            def maxima(par, a, qt, item, pair=None):
                if pair is not None:
                    pe.wait_ge(s_head[a], 96 * pair + 96)
                if item is not None:
                    pe.wait_ge(s_mx, item)
                for kh in range(2):
                    mm = nc.tensor.matmul(mps[:, kh * 512:(kh + 1) * 512], q_hh[:, par, a, qt * P:(qt + 1) * P],
                                          k_hl[:, par, a, kh * 512:(kh + 1) * 512], start=True, stop=True)
                mm.then_inc(s_maxmm, 1)

            def values_of(t):
                for h in range(2):
                    if t >= 2:
                        pe.wait_ge(s_vlo, 2 * (t - 2) + h + 1)
                    nc.tensor.matmul(sps[:, t % 2, h * 512:(h + 1) * 512], xT[:, t * P:(t + 1) * P],
                                     wv[:, h * 512:(h + 1) * 512], start=True, stop=True).then_inc(s_vps, 1)

            def project_early(batch, k, bank):
                x = slice(batch * S + k % 2 * 512, batch * S + k % 2 * 512 + 512)
                nc.tensor.matmul(bank, wqk[:, k // 2, :], xT[:, x], start=True, stop=True).then_inc(s_misc, 1)

            def project(batch, k, job):
                x = slice(batch * S + k % 2 * 512, batch * S + k % 2 * 512 + 512)
                pe.wait_ge(s_used, job)
                nc.tensor.matmul(misc[:], wqk_hi[:, k // 2, :], xT_hi[:, x], start=True, stop=False)
                nc.tensor.matmul(misc[:], wqk_hi[:, k // 2, :], xT_lo[:, x], start=False, stop=False)
                nc.tensor.matmul(misc[:], wqk_lo[:, k // 2, :], xT_hi[:, x], start=False,
                                 stop=True).then_inc(s_misc, 1)

            def turn_maxima(a, job, items):
                pe.wait_ge(s_mx, items)
                pe.wait_ge(s_used, job)
                nc.tensor.transpose(misc[0:TB, 0:P], mx[:, a, :], mem["ident"][:]).then_inc(s_misc, 1)

            def turn_output(par, half, job, units):
                pe.wait_ge(s_oevac, units)
                pe.wait_ge(s_used, job)
                for q in range(4):
                    mm = nc.tensor.transpose(misc[:, q * P:(q + 1) * P], mem["ao"][:, par, 4 * half + q, :],
                                             mem["ident"][:])
                mm.then_inc(s_misc, 1)

            def project_output(par, job, loads):
                pe.wait_ge(s_wo, loads)
                pe.wait_ge(s_used, job)
                for q in range(4):
                    mm = nc.tensor.matmul(misc[:, q * P:(q + 1) * P], aoT[:, q, :], mem["wo"][:, par, :],
                                          start=True, stop=True)
                mm.then_inc(s_misc, 1)

            def values(par, a, c, n, pair):
                half, kk = divmod(c, CH // 2)
                if a == 0 and c == 0:
                    pe.wait_ge(s_v, 16 * pair + 16)
                pe.wait_ge(s_subv, n + 1)
                pe.wait_ge(s_subp, n + 1)
                if kk == 0:
                    pe.wait_ge(s_oevac, 4 * pair + 2 * a + half + 1)
                buf = c % 4
                for kt in range(2):
                    v = vbuf[:, par, 2 * kk + kt, a, :]
                    for q in range(4):
                        w = slice(kt * 512 + q * P, kt * 512 + (q + 1) * P)
                        nc.tensor.matmul(O[:, q, :], ph[:, buf, w], v[:, 0:HD + 1],
                                         start=(kk == 0 and kt == 0 and q == 0), stop=False, skip_group_check=True)
                        nc.tensor.matmul(O[:, q, 0:HD], ph[:, buf, w], v[:, HD + 1:VW],
                                         start=False, stop=False, skip_group_check=True)
                        mm = nc.tensor.matmul(O[:, q, :], pl[:, buf, w], v[:, 0:HD + 1], start=False,
                                              stop=(kk == CH // 2 - 1 and kt == 1 and q == 3), skip_group_check=True)
                mm.then_inc(s_pv, 1)

            pe.wait_ge(s_w, 32)
            pe.wait_ge(s_xT, 16)
            for k in range(4):
                project_early(0, k, p_banks[k])
            pe.wait_ge(s_wv, 16)
            for t in range(T + 2):
                if t < T:
                    values_of(t)
                if P1_TILE <= t < P1_TILE + 4:
                    pe.wait_ge(s_used, 4 + t - P1_TILE)
                    project_early(1, t - P1_TILE, misc[:])
                if t == T + 2 - LEAD_M:
                    pe.wait_ge(s_used, 4)
                    pe.wait_ge(s_ident, 1)
                if t >= T + 2 - LEAD_M:
                    item = t - (T + 2 - LEAD_M)
                    a, qt = divmod(item, TB)
                    maxima(0, a, qt, item, 0 if qt == 0 else None)
                    if item == TB:
                        turn_maxima(0, PRO_MISC - 1, TB)
            pe.wait_ge(s_vlo, 2 * T)
            pe.wait_ge(s_xlo, 1)
            pe.wait_ge(s_init, 1)
            scores(0, 0, 0, None, (0, 0))
            scores(0, 0, 1, None, None)
            scores(0, 0, 2, 2, None)

            with pe.Fori(0, PAIRS // 2) as it:
                for par in range(2):
                    pp = it * 2 + par
                    job = PRO_MISC + MISC * pp
                    for s in range(PCH):
                        n = PCH * pp + s
                        over, t = divmod(s + LEAD_M, PCH)
                        ma, qt = divmod(t, TB)
                        maxima((par + over) % 2, ma, qt, n + LEAD_M, pp + over if qt == 0 else None)
                        over, t = divmod(s + LEAD_S, PCH)
                        sa, sc = divmod(t, CH)
                        scores((par + over) % 2, sa, sc, n + LEAD_S,
                               (pp + over, 2 * (pp + over) + sa) if sc == 0 else None)
                        values(par, s // CH, s % CH, n, pp)
                        if s in JOBS:
                            kind, k = JOBS[s]
                            j = job + job_of_slot[s]
                            if kind == "turn":
                                turn_output(1 - par, k, j, 4 * pp + 1)
                            if kind == "add":
                                project_output(1 - par, j, 16 * pp + 16)
                            if kind == "maxima":
                                turn_maxima(k, j, PCH * pp + (16 if k else 24))
                            if kind == "project":
                                if par == 0 and k == 0:
                                    pe.wait_ge(s_wlo, it + 1)
                                project(par, k, j)
            job = PRO_MISC + MISC * PAIRS
            for half in range(2):
                turn_output(1, half, job + 2 * half, 4 * PAIRS + 1)
                project_output(1, job + 2 * half + 1, 16 * PAIRS + 16)

        @block.scalar
        def _(act):
            def exps(c, n):
                act.wait_ge(s_scores, n + 1)
                buf = q = n if c is None else c
                nc.scalar.activation(p32[:, q % 4, :], sps[:, buf % 2, :], ACT.Exp, bias=EXP_BIAS, scale=SCALE)
                nc.scalar.activation(ph[:, q % 4, :], sps[:, buf % 2, :], ACT.Exp, bias=EXP_BIAS, scale=SCALE).then_inc(s_exp, 1)

            def send_max(par, a, jobs, sent):
                act.wait_ge(s_used, jobs)
                if sent is not None:
                    act.wait_ge(s_negm, sent)
                act.dma_start(q_lm[HD:HD + 1, par, a, :].bitcast(F32),
                              negm[:, a, :].bitcast(F32)).then_inc(s_negm, 16)

            def round_piece(k, job, spread, src=misc[:]):
                if spread is not None and k == 0:
                    for a in range(2):
                        act.wait_ge(s_head[a], spread)
                act.wait_ge(s_misc, job + 1)
                nc.scalar.copy(hi[:, k // 2, k % 2 * 512:(k % 2 + 1) * 512], src).then_inc(s_hi, 1)

            def take_turned(job):
                act.wait_ge(s_misc, job + 1)
                nc.scalar.activation(aoT[:].rearrange("p q t -> p (q t)"), misc[:], ACT.Copy,
                                     scale=vinv[:, 0:1]).then_inc(s_used, 1)

            def round_weights(loads):
                act.wait_ge(s_w, loads)
                nc.scalar.copy(wqk_hi[:], wqk[:]).then_inc(s_whi, 1)

            def high_values(t):
                if t >= V_BUFS:
                    act.wait_ge(s_vout[t % V_BUFS], 16 * (t // V_BUFS))
                for h in range(2):
                    act.wait_ge(s_vps, 2 * t + h + 1)
                    rows = vt[:, t % V_BUFS, h * H // 2:(h + 1) * H // 2, 0:HD]
                    nc.scalar.activation(rows, sps[:, t % 2, h * 512:(h + 1) * 512].rearrange("p (h c) -> p h c", c=HD),
                                         ACT.Copy, scale=vscale[:, 0:1]).then_inc(s_vhi, 1)

            def store_values(t):
                act.wait_ge(s_vlo, 2 * t + 2)
                b, i = divmod(t, TB)
                dst = io["v_dram"][b * H // 2:(b + 1) * H // 2, :, i, :].rearrange("j p c -> p j c")
                act.dma_start(dst, vt[:, t % V_BUFS].rearrange("p (j a) c -> p j (a c)", a=2))\
                    .then_inc(s_vout[t % V_BUFS], 16)

            for k in range(4):
                round_piece(k, k, None, p_banks[k])
            act.wait_ge(s_bound, 3)
            act.wait_ge(s_ones, 1)
            for t in range(T):
                high_values(t)
                if t:
                    store_values(t - 1)
                if P1_TILE <= t < P1_TILE + 4:
                    round_piece(t - P1_TILE, 4 + t - P1_TILE, 96)
                if t == T - 2:
                    send_max(0, 0, PRO_MISC, None)
            store_values(T - 1)
            round_weights(64)
            exps(None, 0)
            exps(None, 1)
            exps(None, 2)
            with act.Fori(0, PAIRS // 2) as it:
                for par in range(2):
                    pp = it * 2 + par
                    for s in range(PCH):
                        exps((s + LEAD_S) % CH, PCH * pp + s + LEAD_S)
                        if s in JOBS and JOBS[s][0] == "project":
                            round_piece(JOBS[s][1], PRO_MISC + MISC * pp + job_of_slot[s], 96 * pp + 192)
                        if s in JOBS and JOBS[s][0] == "turn":
                            take_turned(PRO_MISC + MISC * pp + job_of_slot[s])
                        if par == 1 and s == 8:
                            round_weights(32 * it + 96)
                        if s - 1 in JOBS and JOBS[s - 1][0] == "maxima":
                            a = JOBS[s - 1][1]
                            send_max(par if a else 1 - par, a, PRO_MISC + MISC * pp + job_of_slot[s - 1] + 1,
                                     32 * pp + (16 if a else 32))
            act.wait_ge(s_negm, 16 * (2 * PAIRS + 1))
            for half in range(2):
                take_turned(PRO_MISC + MISC * PAIRS + 2 * half)

        @block.gpsimd
        def _(pool):
            def low_parts(c, n):
                pool.wait_ge(s_exp, n + 1)
                nc.gpsimd.tensor_tensor(pl[:, c % 4, 0:POOL_COLS], p32[:, c % 4, 0:POOL_COLS],
                                        ph[:, c % 4, 0:POOL_COLS], ALU.subtract).then_inc(s_subp, 1)

            nc.gpsimd.memset(mem["ident"][:], 0.0).then_inc(s_zero, 1)
            pool.wait_ge(s_zero, 1)
            nc.gpsimd.affine_select(out=mem["ident"][:], in_=mem["ident"][:], compare_op=ALU.not_equal, fill=1.0,
                                    base=0, pattern=[[-1, P]], channel_multiplier=1).then_inc(s_ident, 1)
            pool.wait_ge(s_top, 2)
            nc.gpsimd.partition_all_reduce(alltops[:], tops[:], P, bass.bass_isa.ReduceOp.max).then_inc(s_alltop, 1)
            nc.gpsimd.memset(mem["ao"][:, 1], 0.0).then_inc(s_oevac, 1)
            pool.wait_ge(s_oevac, 1)
            nc.gpsimd.memset(k_h1[HD:HD + 1].bitcast(F32), 1.0).then_inc(s_init, 1)
            pool.wait_ge(s_init, 1)
            pool.wait_ge(s_x, 16)
            pool.wait_ge(s_bo, 16)
            nc.gpsimd.tensor_tensor(mem["y"][:], mem["y"][:], bo[:].unsqueeze(1).broadcast_to([P, T, D]),
                                    ALU.add).then_inc(s_xbo, 1)
            pool.wait_ge(s_xT, 16)
            nc.gpsimd.tensor_copy(xT_hi[:], xT[:]).then_inc(s_xhi, 1)
            pool.wait_ge(s_xhi, 1)
            nc.gpsimd.tensor_tensor(xT_lo[:], xT[:], xT_hi[:], ALU.subtract).then_inc(s_xlo, 1)
            low_parts(0, 0)
            low_parts(1, 1)
            low_parts(2, 2)
            with pool.Fori(0, PAIRS * PCH // 4) as it:
                for s in range(4):
                    low_parts(s + LEAD_S, it * 4 + s + LEAD_S)

        @block.vector
        def _(dve):
            def reduce_max(slot, qt, item):
                dve.wait_ge(s_maxmm, item + 1)
                nc.vector.tensor_reduce(mx[:, slot, qt:qt + 1], mps[:], AX.X, ALU.max).then_inc(s_mx, 1)

            def low_parts(c, n):
                dve.wait_ge(s_exp, n + 1)
                nc.vector.tensor_tensor(pl[:, c % 4, POOL_COLS:], p32[:, c % 4, POOL_COLS:],
                                        ph[:, c % 4, POOL_COLS:], ALU.subtract).then_inc(s_subv, 1)

            def rest_of_weights(n):
                dve.wait_ge(s_whi, n)
                nc.vector.tensor_tensor(wqk_lo[:], wqk[:], wqk_hi[:], ALU.subtract).then_inc(s_wlo, 1)

            def low_values(t):
                for h in range(2):
                    dve.wait_ge(s_vhi, 2 * t + h + 1)
                    rows = vt[:, t % V_BUFS, h * H // 2:(h + 1) * H // 2, :]
                    nc.vector.scalar_tensor_tensor(
                        out=rows[:, :, HD + 1:VW],
                        in0=sps[:, t % 2, h * 512:(h + 1) * 512].rearrange("p (h c) -> p h c", c=HD),
                        scalar=vscale[:, 0:1], in1=rows[:, :, 0:HD], op0=ALU.mult, op1=ALU.subtract).then_inc(s_vlo, 1)

            def rest_of_piece(k, job, pieces, src=misc[:]):
                dve.wait_ge(s_hi, pieces)
                cols = slice(k % 2 * 512, (k % 2 + 1) * 512)
                nc.vector.tensor_tensor(lo[:, k // 2, cols], src, hi[:, k // 2, cols],
                                        ALU.subtract).then_inc(s_used, 1)

            def negate_maxima(a, job, sent):
                if sent is not None:
                    dve.wait_ge(s_negm, sent)
                dve.wait_ge(s_misc, job + 1)
                nc.vector.tensor_scalar(negm[:, a, :], misc[0:TB, 0:P], -1.0, None, ALU.mult).then_inc(s_used, 1)

            def add_output(batch, half, job):
                dve.wait_ge(s_misc, job + 1)
                y = mem["y"][:, batch * TB + 4 * half:batch * TB + 4 * half + 4, :]
                nc.vector.tensor_tensor(y, misc[:].rearrange("p (q d) -> p q d", q=4), y, ALU.add).then_inc(s_used, 1)

            def normalise(par, a, half, unit):
                dve.wait_ge(s_pv, 4 * unit + 4)
                nc.vector.reciprocal(rec[:], O[:, :, HD]).then_inc(s_rec, 1)
                dve.wait_ge(s_rec, unit + 1)
                nc.vector.tensor_tensor(mem["ao"][:, par, 4 * half:4 * half + 4, a * HD:(a + 1) * HD], O[:, :, 0:HD],
                                        rec[:].unsqueeze(2).broadcast_to([P, 4, HD]),
                                        ALU.mult).then_inc(s_oevac, 1)

            nc.vector.memset(vt[:, :, :, HD:HD + 1], 1.0).then_inc(s_ones, 1)
            dve.wait_ge(s_xT, 16)
            nc.vector.tensor_reduce(tops[:, 0:1], xT[:], AX.X, ALU.max, apply_absolute_value=True).then_inc(s_top, 1)
            dve.wait_ge(s_wv, 16)
            nc.vector.tensor_reduce(tops[:, 1:2], wv[:], AX.X, ALU.max, apply_absolute_value=True).then_inc(s_top, 1)
            for k in range(4):
                rest_of_piece(k, k, k + 1, p_banks[k])
            dve.wait_ge(s_alltop, 1)
            nc.vector.scalar_tensor_tensor(out=bound[:], in0=alltops[:, 0:1], scalar=D / V_TOP,
                                           in1=alltops[:, 1:2], op0=ALU.mult, op1=ALU.mult).then_inc(s_bound, 1)
            dve.wait_ge(s_bound, 1)
            nc.vector.tensor_scalar(vinv[:], bound[:], 1e-30, None, ALU.max).then_inc(s_bound, 1)
            dve.wait_ge(s_bound, 2)
            nc.vector.reciprocal(vscale[:], vinv[:]).then_inc(s_bound, 1)
            dve.wait_ge(s_bound, 3)
            dve.wait_ge(s_ones, 1)
            for t in range(T + 2):
                if t < T:
                    low_values(t)
                if P1_TILE <= t < P1_TILE + 4:
                    rest_of_piece(t - P1_TILE, 4 + t - P1_TILE, 5 + t - P1_TILE)
                if t >= T + 2 - LEAD_M:
                    item = t - (T + 2 - LEAD_M)
                    reduce_max(item // TB, item % TB, item)
                    if item == TB:
                        negate_maxima(0, PRO_MISC - 1, None)
            dve.wait_ge(s_xbo, 1)
            rest_of_weights(1)
            low_parts(0, 0)
            with dve.Fori(0, PAIRS // 2) as it:
                for par in range(2):
                    pp = it * 2 + par
                    job = PRO_MISC + MISC * pp
                    for s in range(PCH):
                        n = PCH * pp + s
                        ma, qt = divmod((s + LEAD_M) % PCH, TB)
                        if s in (4, 8, 12):
                            u = s // 4 - 1
                            normalise(par, u // 2, u % 2, 4 * pp + u)
                        kind, k = JOBS.get(s - 1, (None, 0))
                        j = job + job_of_slot.get(s - 1, 0)
                        if kind == "maxima":
                            negate_maxima(k, j, 32 * pp + 16)
                        if kind == "add" and s in JOBS:
                            add_output(1 - par, k, j)
                        reduce_max(ma, qt, n + LEAD_M)
                        if kind == "add" and s not in JOBS:
                            add_output(1 - par, k, j)
                        if kind == "project":
                            rest_of_piece(k, j, 4 * pp + 9 + k)
                        if par == 1 and s == 9:
                            rest_of_weights(it + 2)
                        low_parts((s + 1) % CH, n + 1)
                    normalise(par, 1, 1, 4 * pp + 3)
            job = PRO_MISC + MISC * PAIRS
            for half in range(2):
                add_output(B - 1, half, job + 2 * half + 1)


def norm_statistics(nc, k, src, stats, mv, s_var, then):
    tiles = range(4 * k, 4 * k + 4)
    for t in tiles:
        ins = nc.vector.bn_stats(stats[:, t, :], src[:, t, :])
    then(ins)
    for t in tiles:
        ins = nc.vector.bn_aggr(mv[:, t, :], stats[:, t, :])
    then(ins)
    nc.vector.tensor_scalar(mv[:, 4 * k:4 * k + 4, 1:2], mv[:, 4 * k:4 * k + 4, 1:2], EPS, None,
                            ALU.add).then_inc(s_var, 1)


def norm_factors(nc, dve, k, n, mv, rstd, shift, s_root, s_shifted, then):
    g = slice(4 * k, 4 * k + 4)
    dve.wait_ge(s_root, n + 1)
    then(nc.vector.reciprocal(rstd[:, g], rstd[:, g]))
    nc.vector.scalar_tensor_tensor(out=shift[:, g], in0=mv[:, g, 0], scalar=-1.0, in1=rstd[:, g],
                                   op0=ALU.mult, op1=ALU.mult).then_inc(s_shifted, 1)


def norm_root(nc, act, k, n, mv, rstd, s_var, s_root):
    act.wait_ge(s_var, n + 1)
    nc.scalar.activation(rstd[:, 4 * k:4 * k + 4], mv[:, 4 * k:4 * k + 4, 1], ACT.Sqrt).then_inc(s_root, 1)


def norm_apply(nc, act, k, n, src, rstd, shift, s_shifted, s_normed):
    act.wait_ge(s_shifted, n + 1)
    for t in range(4 * k, 4 * k + 4):
        nc.scalar.activation(src[:, t, :], src[:, t, :], ACT.Identity, bias=shift[:, t:t + 1],
                             scale=rstd[:, t:t + 1]).then_inc(s_normed, 1)


def mixture(nc, io, mem):
    BL = T // 4
    NC = len(F_CHUNKS)
    UNITS = BL * 2
    with ExitStack() as ctx:
        sb = lambda name, shape, dt: ctx.enter_context(nc.sbuf_tensor(name, shape, dt))
        sem = lambda name: ctx.enter_context(nc.semaphore(name))
        y = mem["y"]
        stats = sb("stats", [P, T, 6], F32)
        mv = sb("mv", [P, T, 2], F32)
        rstd = sb("rstd", [P, T], F32)
        shift = sb("shift", [P, T], F32)
        wg = sb("wg", [P, 3 * E], F32)
        mixed = sb("mixed", [P, T, 3 * E], F32)
        prod = sb("prod", [P, T, E, E], F32)
        pv = sb("pv", [P, T, E, E], F32)
        g = sb("g", [P, 9, T, E], F32)
        one = sb("one", [P, 5, T], F32)
        rank = sb("rank", [P, E], F32)
        gate = sb("gate", [P, T, E], F32)
        x1T = sb("x1T", [P, T * P], F32)
        x_hi = sb("x_hi", [P, T * P], F32R)
        x_lo = sb("x_lo", [P, T * P], F32R)
        w1 = sb("w1", [P, 2, 2 * F], F32)
        w1_hi = sb("w1_hi", [P, 2, 2 * F], F32R)
        w1_lo = sb("w1_lo", [P, 2, 2 * F], F32R)
        w2 = sb("w2", [P, 2, NC, D], F32)
        silu = sb("silu", [P, 3, 512], F32)
        he = sb("he", [P, 3, 512], F32)
        part = sb("part", [P, 4, D], F32)
        aps = ctx.enter_context(nc.psum_tensor("aps", [P, 3, 512], F32))
        gps = ctx.enter_context(nc.psum_tensor("gps", [P, 3, 512], F32))
        yps = ctx.enter_context(nc.psum_tensor("yps", [P, 2, 512], F32))
        tps = yps
        mps = gps[:, 2, 0:T * 3 * E]
        s_w = [sem("s_we0"), sem("s_we1")]
        s_wg, s_chain = sem("s_wg"), sem("s_chain")
        s_var, s_root, s_shifted, s_normed = (sem(n) for n in ("s_var", "s_root", "s_shifted", "s_normed"))
        s_turn, s_mixmm, s_mixed = sem("s_turn"), sem("s_mixmm"), sem("s_mixed")
        s_shift, s_gexp, s_out = sem("s_shift"), sem("s_gexp"), sem("s_out")
        s_taken, s_xlo, s_whi, s_wlo = sem("s_taken"), sem("s_xlo"), sem("s_whi"), sem("s_wlo")
        s_h, s_silu, s_he, s_y, s_part, s_add = (sem(n) for n in ("s_h", "s_silu", "s_he", "s_y", "s_part", "s_add"))
        block = ctx.enter_context(nc.Block())

        @block.sync
        def _(sp):
            def ready(x):
                return sp.snap(sp.to_reg(x))

            def load(e, par):
                sp.dma_start(w1[:, par, :], io["w1T"][bass.ds(e, 1), :, :].rearrange("o h f -> h (o f)"))\
                    .then_inc(s_w[par], 16)
                sp.dma_start(w2[:, par, 0:2, :], io["w2T"][bass.ds(e, 1), 0:2 * P, :].rearrange(
                    "o (c p) h -> p (o c) h", p=P)).then_inc(s_w[par], 16)
                sp.dma_start(w2[0:F - 2 * P, par, 2, :], io["w2T"][bass.ds(e, 1), 2 * P:F, :].rearrange(
                    "o p h -> (o p) h")).then_inc(s_w[par], 16)

            sp.dma_start(wg[:], io["wqkvT"]).then_inc(s_wg, 16)
            load(0, 0)
            load(1, 1)
            with sp.Fori(0, E // 2) as it:
                for par in range(2):
                    expert = ready((it * 2 + par + 2) % E)
                    used = ready(it * UNITS + (par + 1) * BL)
                    loaded = ready(it * 48 + 48)
                    sp.wait_ge(s_y, used)
                    sp.wait_ge(s_w[par], loaded)
                    load(expert, par)
            for par in range(2):
                sp.wait_ge(s_w[par], 48 * (E // 2 + 1))
            out = io["out"].rearrange("b (t p) d -> p (b t) d", p=P)
            for k in range(T // 4):
                sp.wait_ge(s_normed, T + 4 * k + 4)
                sp.dma_start(out[:, 4 * k:4 * k + 4, :], y[:, 4 * k:4 * k + 4, :]).then_inc(s_out, 16)
            sp.wait_ge(s_out, 16 * (T // 4))

        @block.tensor
        def _(pe):
            def turn(k):
                if k >= 2:
                    pe.wait_ge(s_taken, k - 1)
                for t in range(4 * k, 4 * k + 4):
                    pe.wait_ge(s_normed, t + 1)
                    tr = nc.tensor.transpose(tps[:, k % 2, t % 4 * P:(t % 4 + 1) * P], y[:, t, :], mem["ident"][:])
                tr.then_inc(s_turn, 1)

            def mix(k):
                pe.wait_ge(s_taken, k + 1)
                for t in range(4 * k, 4 * k + 4):
                    mm = nc.tensor.matmul(mps[:, t * 3 * E:(t + 1) * 3 * E], x1T[:, t * P:(t + 1) * P], wg[:],
                                          start=True, stop=True)
                if k == T // 4 - 1:
                    mm.then_inc(s_mixmm, 1)

            turn(0)
            turn(1)
            pe.wait_ge(s_wg, 16)
            for k in range(T // 4):
                mix(k)
                if k + 2 < T // 4:
                    turn(k + 2)

            def hidden(it, k):
                over, t = divmod(k, UNITS * NC)
                u, c = divmod(t, NC)
                par, bl = divmod(u, BL)
                if bl == 0 and c == 0:
                    pe.wait_ge(s_wlo, (it + over) * 2 + par + 1)
                    pe.wait_ge(s_w[par], (it + over) * 48 + 48)
                off, n = F_CHUNKS[c]
                x = slice(bl * 512, (bl + 1) * 512)
                for out, o in ((aps, off), (gps, F + off)):
                    w = slice(o, o + n)
                    nc.tensor.matmul(out[0:n, t % 3, :], w1_hi[:, par, w], x_hi[:, x], start=True, stop=False)
                    nc.tensor.matmul(out[0:n, t % 3, :], w1_hi[:, par, w], x_lo[:, x], start=False, stop=False)
                    mm = nc.tensor.matmul(out[0:n, t % 3, :], w1_lo[:, par, w], x_hi[:, x], start=False, stop=True)
                mm.then_inc(s_h, 1)

            def down(it, k):
                u, c = divmod(k, NC)
                pe.wait_ge(s_he, it * (UNITS * NC) + k + 1)
                n = F_CHUNKS[c][1]
                for q in range(4):
                    mm = nc.tensor.matmul(yps[:, u % 2, q * D:(q + 1) * D], he[0:n, k % 3, q * P:(q + 1) * P],
                                          w2[0:n, u // BL, c, :], start=(c == 0 and q == 0),
                                          stop=(c == NC - 1 and q == 3), skip_group_check=True)
                if c == NC - 1:
                    mm.then_inc(s_y, 1)

            pe.wait_ge(s_xlo, BL)
            hidden(0, 0)
            hidden(0, 1)
            pe.wait_ge(s_mixed, 1)
            with pe.Fori(0, E // 2) as it:
                for k in range(UNITS * NC):
                    hidden(it, k + 2)
                    down(it, k)

        @block.scalar
        def _(act):
            def round_w1(par, n):
                act.wait_ge(s_w[par], n)
                nc.scalar.copy(w1_hi[:, par, :], w1[:, par, :]).then_inc(s_whi, 1)

            def take_turned(k):
                cols = slice(k * 512, (k + 1) * 512)
                act.wait_ge(s_turn, k + 1)
                nc.scalar.copy(x1T[:, cols], tps[:, k % 2, :])
                nc.scalar.copy(x_hi[:, cols], tps[:, k % 2, :]).then_inc(s_taken, 1)

            norm_root(nc, act, 0, 0, mv, rstd, s_var, s_root)
            for k in range(T // 4):
                if k + 1 < T // 4:
                    norm_root(nc, act, k + 1, k + 1, mv, rstd, s_var, s_root)
                norm_apply(nc, act, k, k, y, rstd, shift, s_shifted, s_normed)
                if k:
                    take_turned(k - 1)
            take_turned(T // 4 - 1)
            act.wait_ge(s_mixmm, 1)
            nc.scalar.copy(mixed[:].rearrange("p t c -> p (t c)"), mps).then_inc(s_mixed, 1)

            def silus(it, k):
                t = k % (UNITS * NC)
                n = F_CHUNKS[t % NC][1]
                act.wait_ge(s_h, it * (UNITS * NC) + k + 1)
                nc.scalar.activation(silu[0:n, t % 3, :], aps[0:n, t % 3, :], ACT.Silu).then_inc(s_silu, 1)

            silus(0, 0)
            act.wait_ge(s_shift, 1)
            nc.scalar.activation(prod[:], prod[:], ACT.Exp).then_inc(s_gexp, 1)
            silus(0, 1)
            act.wait_ge(s_shift, 2)
            nc.scalar.activation(g[:, 4], g[:, 4], ACT.Exp).then_inc(s_gexp, 1)
            with act.Fori(0, E // 2) as it:
                for k in range(UNITS * NC):
                    silus(it, k + 2)
                    if k == BL // 2 * NC:
                        round_w1(1, it * 48 + 48)
                    if k == (BL + BL // 2) * NC:
                        round_w1(0, it * 48 + 96)
            norm_root(nc, act, 0, T // 4, mv, rstd, s_var, s_root)
            for k in range(T // 4):
                if k + 1 < T // 4:
                    norm_root(nc, act, k + 1, T // 4 + k + 1, mv, rstd, s_var, s_root)
                norm_apply(nc, act, k, T // 4 + k, y, rstd, shift, s_shifted, s_normed)

        @block.gpsimd
        def _(pool):
            def rest_of_w1(par, n):
                pool.wait_ge(s_whi, n)
                nc.gpsimd.tensor_tensor(w1_lo[:, par, :], w1[:, par, :], w1_hi[:, par, :],
                                        ALU.subtract).then_inc(s_wlo, 1)

            pool.wait_ge(s_w[0], 48)
            nc.gpsimd.tensor_copy(w1_hi[:, 0, :], w1[:, 0, :]).then_inc(s_whi, 1)
            rest_of_w1(0, 1)

            with pool.Fori(0, E // 2) as it:
                rest_of_w1(1, it * 2 + 2)
                rest_of_w1(0, it * 2 + 3)

        @block.vector
        def _(dve):
            steps = [0]

            def then(ins):
                steps[0] += 1
                ins.then_inc(s_chain, 1)
                dve.wait_ge(s_chain, steps[0])

            def gated(it, k):
                t = k % (UNITS * NC)
                n = F_CHUNKS[t % NC][1]
                dve.wait_ge(s_silu, it * (UNITS * NC) + k + 1)
                nc.vector.tensor_tensor(he[0:n, t % 3, :], silu[0:n, t % 3, :], gps[0:n, t % 3, :],
                                        ALU.mult).then_inc(s_he, 1)

            def add_unit(it, u):
                par, bl = divmod(u, BL)
                unit = it * UNITS + u
                dve.wait_ge(s_y, unit + 1)
                weight = gate[:, bl * 4:(bl + 1) * 4, bass.ds(it * 2 + par, 1)].broadcast_to([P, 4, D])
                nc.vector.tensor_tensor(part[:], yps[:, u % 2, :].rearrange("p (q d) -> p q d", q=4), weight,
                                        ALU.mult).then_inc(s_part, 1)
                dve.wait_ge(s_part, unit + 1)
                rows = y[:, bl * 4:(bl + 1) * 4, :]
                nc.vector.tensor_tensor(rows, rows, part[:], ALU.add).then_inc(s_add, 1)

            def split_x1(k):
                cols = slice(k * 512, (k + 1) * 512)
                dve.wait_ge(s_taken, k + 1)
                nc.vector.tensor_tensor(x_lo[:, cols], x1T[:, cols], x_hi[:, cols], ALU.subtract).then_inc(s_xlo, 1)

            norm_statistics(nc, 0, y, stats, mv, s_var, then)
            for k in range(T // 4):
                if k + 1 < T // 4:
                    norm_statistics(nc, k + 1, y, stats, mv, s_var, then)
                norm_factors(nc, dve, k, k, mv, rstd, shift, s_root, s_shifted, then)
            for k in range(T // 4):
                split_x1(k)
            for e in range(E):
                last = nc.vector.memset(rank[:, e:e + 1], float(E - e))
            then(last)
            q, k, v = (mixed[:, :, i * E:(i + 1) * E] for i in range(3))
            full = [P, T, E, E]
            rows = lambda x: x.unsqueeze(3).broadcast_to(full)
            cols = lambda x: x.unsqueeze(2).broadcast_to(full)
            dve.wait_ge(s_mixed, 1)
            then(nc.vector.tensor_tensor(prod[:], rows(q), cols(k), ALU.mult))
            then(nc.vector.tensor_reduce(g[:, 0], prod[:], AX.X, ALU.max))
            nc.vector.tensor_tensor(prod[:], prod[:], rows(g[:, 0]), ALU.subtract).then_inc(s_shift, 1)
            gated(0, 0)
            dve.wait_ge(s_gexp, 1)
            nc.vector.tensor_tensor(pv[:], prod[:], cols(v), ALU.mult)
            then(nc.vector.tensor_reduce(g[:, 1], prod[:], AX.X, ALU.add))
            nc.vector.tensor_reduce(g[:, 2], pv[:], AX.X, ALU.add)
            then(nc.vector.reciprocal(g[:, 3], g[:, 1]))
            then(nc.vector.tensor_tensor(g[:, 3], g[:, 2], g[:, 3], ALU.mult))
            each = lambda x: x.unsqueeze(2).broadcast_to([P, T, E])
            ranks = rank[:].unsqueeze(1).broadcast_to([P, T, E])
            then(nc.vector.tensor_reduce(one[:, 0, :], g[:, 3], AX.X, ALU.max))
            nc.vector.tensor_tensor(g[:, 4], g[:, 3], each(one[:, 0, :]), ALU.subtract).then_inc(s_shift, 1)

            def largest(logits, top, first, hot, scratch):
                then(nc.vector.tensor_tensor(scratch, logits, each(top), ALU.is_equal))
                then(nc.vector.tensor_tensor(scratch, scratch, ranks, ALU.mult))
                then(nc.vector.tensor_reduce(first, scratch, AX.X, ALU.max))
                then(nc.vector.tensor_tensor(hot, ranks, each(first), ALU.is_equal))

            largest(g[:, 3], one[:, 0, :], one[:, 1, :], g[:, 5], g[:, 6])
            then(nc.vector.scalar_tensor_tensor(out=g[:, 7], in0=g[:, 5], scalar=-3e38, in1=g[:, 3],
                                                op0=ALU.mult, op1=ALU.add))
            gated(0, 1)
            then(nc.vector.tensor_reduce(one[:, 2, :], g[:, 7], AX.X, ALU.max))
            largest(g[:, 7], one[:, 2, :], one[:, 3, :], g[:, 8], g[:, 6])
            then(nc.vector.tensor_tensor(g[:, 5], g[:, 5], g[:, 8], ALU.add))
            dve.wait_ge(s_gexp, 2)
            then(nc.vector.tensor_tensor(g[:, 6], g[:, 4], g[:, 5], ALU.mult))
            then(nc.vector.tensor_reduce(one[:, 4, :], g[:, 6], AX.X, ALU.add))
            then(nc.vector.reciprocal(one[:, 3, :], one[:, 4, :]))
            then(nc.vector.tensor_tensor(gate[:], g[:, 6], each(one[:, 3, :]), ALU.mult))
            with dve.Fori(0, E // 2) as it:
                for k in range(UNITS * NC):
                    gated(it, k + 2)
                    if k % NC == NC - 1:
                        add_unit(it, k // NC)
            dve.wait_ge(s_add, E * BL)
            norm_statistics(nc, 0, y, stats, mv, s_var, then)
            for k in range(T // 4):
                if k + 1 < T // 4:
                    norm_statistics(nc, k + 1, y, stats, mv, s_var, then)
                norm_factors(nc, dve, k, T // 4 + k, mv, rstd, shift, s_root, s_shifted, then)


def bass_transformer_layer_moe(nc, x, xT, Wq, Wk, Wv, Wo, bo, wqkvT, w1T, w2T, out):
    io = dict(x=x, xT=xT, Wq=Wq, Wk=Wk, Wv=Wv, Wo=Wo, bo=bo, wqkvT=wqkvT, w1T=w1T, w2T=w2T, out=out)
    io["v_dram"] = nc.dram_tensor("v_dram", [PAIRS, P, TB, 2 * VW], F16, kind="Internal").ap()
    with ExitStack() as ctx:
        sb = lambda name, shape, dt: ctx.enter_context(nc.sbuf_tensor(name, shape, dt))
        mem = {
            "ident": sb("ident", [P, P], F32),
            "y": sb("y", [P, T, D], F32),
            "ao": sb("ao", [P, 2, TB, P], F32),
            "wo": sb("wo", [P, 2, D], F32),
        }
        attention(nc, io, mem)
        mixture(nc, io, mem)


def kernel(L0_attn_x, L0_attn_Wq, L0_attn_Wk, L0_attn_Wv, L0_attn_Wo, L0_attn_bo, L0_ffn_wqkv, L0_ffn_w1, L0_ffn_w2):
    import numpy as np
    import concourse.bacc as bacc
    from concourse.bass_utils import run_bass_kernel_spmd

    x = np.ascontiguousarray(L0_attn_x)
    ins = {
        "x": x,
        "xT": np.ascontiguousarray(x.reshape(B * S, D).T),
        "Wq": L0_attn_Wq, "Wk": L0_attn_Wk, "Wv": L0_attn_Wv, "Wo": L0_attn_Wo, "bo": L0_attn_bo,
        "wqkvT": np.ascontiguousarray(np.asarray(L0_ffn_wqkv).T),
        "w1T": np.ascontiguousarray(np.asarray(L0_ffn_w1).transpose(0, 2, 1)),
        "w2T": np.ascontiguousarray(np.asarray(L0_ffn_w2).transpose(0, 2, 1)),
    }
    nc = bacc.Bacc("TRN2", target_bir_lowering=False, num_devices=1)
    arrays, args = {}, []
    for name, a in ins.items():
        a = np.ascontiguousarray(a)
        arrays[f"in_{name}"] = a
        args.append(nc.dram_tensor(f"in_{name}", a.shape, mybir.dt.from_np(a.dtype), kind="ExternalInput").ap())
    args.append(nc.dram_tensor("out_0", (B, S, D), F32, kind="ExternalOutput").ap())
    bass_transformer_layer_moe(nc, *args)
    r = run_bass_kernel_spmd(nc, [arrays], core_ids=[0])
    return r.results[0]["out_0"]
```

```python
from contextlib import ExitStack

import concourse.bass as bass
from concourse import mybir

ALU = mybir.AluOpType
ACT = mybir.ActivationFunctionType
AX = mybir.AxisListType
F32 = mybir.dt.float32
F32R = mybir.dt.float32r
F16 = mybir.dt.float16

P = 128
B, S, D = 2, 1024, 128
H, HD = 16, 64
E, F = 8, 352
T = B * S // P
TB = S // P
PAIRS = B * H // 2
VW = 2 * HD + 1
EPS = 1e-5
SCALE = HD ** -0.5
EXP_BIAS = 4.0
V_TOP = 32768.0
POOL_COLS = 896

CH = 8
PCH = 2 * CH
LEAD_S = 3
LEAD_M = 14
PRO_MISC = 9
P1_TILE = 8
V_BUFS = 4
JOBS = {1: ("maxima", 1), 2: ("project", 0), 4: ("project", 1), 5: ("project", 2), 7: ("project", 3),
        9: ("maxima", 0), 10: ("turn", 0), 11: ("add", 0), 12: ("turn", 1), 13: ("add", 1)}
MISC = len(JOBS)


def jobs_of(last, par):
    left = [(slot, kind, k) for slot, (kind, k) in JOBS.items()
            if not (last and (kind == "project" or (par == 1 and (kind, k) == ("maxima", 0))))]
    return {slot: (kind, k, number) for number, (slot, kind, k) in enumerate(left)}


def first_job(last, pp, par):
    return PRO_MISC + MISC * pp - (MISC - len(jobs_of(last, 0)) if par == 1 else 0)


def within(last, par, step):
    return not (last and par == 1 and step >= PCH)


F_CHUNKS = [(0, 128), (128, 128), (256, 96)]


def attention(nc, io, mem):
    with ExitStack() as ctx:
        sb = lambda name, shape, dt: ctx.enter_context(nc.sbuf_tensor(name, shape, dt))
        sem = lambda name: ctx.enter_context(nc.semaphore(name))
        xT = sb("xT", [P, T * P], F32)
        wv = sb("wv", [P, H * HD], F32)
        bo = sb("bo", [P, D], F32)
        tops = sb("tops", [P, 2], F32)
        alltops = sb("alltops", [P, 2], F32)
        bound = sb("bound", [P, 1], F32)
        vinv = mem["vinv"]
        vscale = sb("vscale", [P, 1], F32)
        vt = sb("vt", [P, V_BUFS, H, VW], F16)
        wqk = sb("wqk", [P, 2, P], F32)
        wqk_hi = sb("wqk_hi", [P, 2, P], F32R)
        wqk_lo = sb("wqk_lo", [P, 2, P], F32R)
        xT_hi = sb("xT_hi", [P, T * P], F32R)
        xT_lo = sb("xT_lo", [P, T * P], F32R)
        hi = sb("hi", [P, 2, S], F32R)
        lo = sb("lo", [P, 2, S], F32R)
        q_hh = sb("q_hh", [P, 2, 2, S], F32R)
        q_lm = sb("q_lm", [P, 2, 2, S], F32R)
        k_hl = sb("k_hl", [P, 2, 2, S], F32R)
        k_h1 = sb("k_h1", [P, 2, 2, S], F32R)
        vbuf = sb("vbuf", [P, 2, TB, 2, VW], F16)
        mx = sb("mx", [P, 2, TB], F32)
        negm = sb("negm", [TB, 2, P], F32R)
        p32 = sb("p32", [P, 4, 1024], F32)
        ph = sb("ph", [P, 4, 1024], F16)
        pl = sb("pl", [P, 4, 1024], F16)
        rec = sb("rec", [P, 4], F32)
        aoT = sb("aoT", [P, 4, P], F32)
        sps = ctx.enter_context(nc.psum_tensor("sps", [P, 2, 1024], F32))
        mps = ctx.enter_context(nc.psum_tensor("mps", [P, 1024], F32))
        ops = ctx.enter_context(nc.psum_tensor("ops", [P, 512], F32))
        misc = ctx.enter_context(nc.psum_tensor("misc", [P, 512], F32))
        O = ops[:, 0:4 * (HD + 1)].rearrange("p (q c) -> p q c", c=HD + 1)

        p_banks = [misc[:], ops[:], mps[:, 0:512], mps[:, 512:1024]]

        s_x, s_xT, s_wv, s_bo = sem("s_x"), sem("s_xT"), sem("s_wv"), sem("s_bo")
        s_top, s_alltop, s_bound = sem("s_top"), sem("s_alltop"), sem("s_bound")
        s_zero, s_ident, s_ones, s_xbo = sem("s_zero"), sem("s_ident"), sem("s_ones"), sem("s_xbo")
        s_vps, s_vhi, s_vlo = sem("s_vps"), sem("s_vhi"), sem("s_vlo")
        s_vout = [sem(f"s_vout{k}") for k in range(V_BUFS)]
        s_w, s_v, s_wo, s_negm = sem("s_w"), sem("s_v"), sem("s_wo"), sem("s_negm")
        s_head = [sem("s_head0"), sem("s_head1")]
        s_scores, s_maxmm, s_misc, s_pv = sem("s_scores"), sem("s_maxmm"), sem("s_misc"), sem("s_pv")
        s_exp, s_hi = sem("s_exp"), sem("s_hi")
        s_mx, s_subv, s_used, s_oevac = sem("s_mx"), sem("s_subv"), sem("s_used"), sem("s_oevac")
        s_whi, s_wlo, s_xhi, s_xlo = sem("s_whi"), sem("s_wlo"), sem("s_xhi"), sem("s_xlo")
        s_rec, s_init, s_subp = sem("s_rec"), sem("s_init"), sem("s_subp")
        block = ctx.enter_context(nc.Block())

        @block.sync
        def _(sp):
            def ready(x):
                return sp.snap(sp.to_reg(x))

            def load_projection(pair_of_batch):
                column = pair_of_batch * P
                sp.dma_start(wqk[:, 0, :], io["Wq"][:, bass.ds(column, P)]).then_inc(s_w, 16)
                sp.dma_start(wqk[:, 1, :], io["Wk"][:, bass.ds(column, P)]).then_inc(s_w, 16)

            def load_values(row, par):
                sp.dma_start(vbuf[:, par], io["v_dram"][bass.ds(row, 1), :, :, :].rearrange(
                    "o p t (a c) -> p (o t) a c", a=2)).then_inc(s_v, 16)

            def spread_head(par, a):
                r = slice(HD * a, HD * a + HD)
                for dst, src in ((q_hh[0:HD, par, a, :], hi[r, 0, :]), (q_hh[HD:P, par, a, :], hi[r, 0, :]),
                                 (q_lm[0:HD, par, a, :], lo[r, 0, :]), (k_hl[0:HD, par, a, :], hi[r, 1, :]),
                                 (k_hl[HD:P, par, a, :], lo[r, 1, :]), (k_h1[0:HD, par, a, :], hi[r, 1, :])):
                    sp.dma_start(dst.bitcast(F32), src.bitcast(F32)).then_inc(s_head[a], 16)

            load_projection(0)
            sp.dma_start(xT[:], io["xT"]).then_inc(s_xT, 16)
            sp.dma_start(wv[:], io["Wv"]).then_inc(s_wv, 16)
            sp.dma_start(mem["y"][:], io["x"].rearrange("b (t p) d -> p (b t) d", p=P)).then_inc(s_x, 16)
            sp.dma_start(bo[:], io["bo"].rearrange("(a d) -> a d", a=1).broadcast_to([P, D])).then_inc(s_bo, 16)
            sp.dma_start(mem["wo"][:, 1, :], io["Wo"][0:P, :]).then_inc(s_wo, 16)
            sp.wait_ge(s_used, 4)
            spread_head(0, 0)
            spread_head(0, 1)
            for k in range(V_BUFS):
                sp.wait_ge(s_vout[k], 16 * TB // V_BUFS)
            load_values(0, 0)
            sp.wait_ge(s_used, 8)
            load_projection(1)
            for a in range(2):
                sp.wait_ge(s_head[a], 96)
                spread_head(1, a)
            for k in range(V_BUFS):
                sp.wait_ge(s_vout[k], 16 * T // V_BUFS)
            def turn_of_pairs(it, last, ready):
                if not last:
                    pair_of_batch = ready((it + 2) % (H // 2))
                    weights_split = ready(it + 1)
                    weights_loaded = ready(32 * it + 64)
                    sp.wait_ge(s_wlo, weights_split)
                    sp.wait_ge(s_w, weights_loaded)
                    load_projection(pair_of_batch)
                for par in range(2):
                    pp = it * 2 + par
                    next_values = ready(it + H // 2) if par == 0 else ready((it + 1) % (H // 2))
                    wo_row = ready(it * P)
                    values_loaded = ready(16 * pp + 16)
                    values_used = ready(PCH * pp + LEAD_S + 1)
                    wo_loaded = ready(16 * pp + 16)
                    wo_used = ready(first_job(last, pp, par))
                    pair_split = ready(PRO_MISC + MISC * pp + 5)
                    head_scored = [ready(PCH * pp + CH), ready(PCH * pp + PCH)]
                    head_spread = ready(96 * pp + 192)
                    if within(last, par, PCH):
                        sp.wait_ge(s_v, values_loaded)
                        sp.wait_ge(s_scores, values_used)
                        load_values(next_values, 1 - par)
                    sp.wait_ge(s_misc, wo_used)
                    sp.wait_ge(s_wo, wo_loaded)
                    sp.dma_start(mem["wo"][:, par, :], io["Wo"][bass.ds(wo_row, P), :]).then_inc(s_wo, 16)
                    if last:
                        continue
                    sp.wait_ge(s_used, pair_split)
                    sp.wait_ge(s_scores, head_scored[0])
                    sp.wait_ge(s_head[0], head_spread)
                    spread_head(par, 0)
                    sp.wait_ge(s_scores, head_scored[1])
                    sp.wait_ge(s_head[1], head_spread)
                    spread_head(par, 1)

            with sp.Fori(0, PAIRS // 2 - 1) as it:
                turn_of_pairs(it, False, ready)
            turn_of_pairs(PAIRS // 2 - 1, True, lambda x: x)
            for a in range(2):
                sp.wait_ge(s_head[a], 96 * PAIRS)
            sp.wait_ge(s_v, 16 * PAIRS)
            sp.wait_ge(s_w, 32 * (PAIRS // 2 + 1))
            sp.wait_ge(s_wo, 16 * PAIRS + 16)

        @block.tensor
        def _(pe):
            def scores(par, a, c, n, first_of_head):
                half, kk = divmod(c, CH // 2)
                q = slice(half * 512, half * 512 + 512)
                if first_of_head is not None:
                    pair, head = first_of_head
                    pe.wait_ge(s_head[a], 96 * pair + 96)
                    pe.wait_ge(s_negm, 16 * head + 16)
                buf = c % 2
                if n is not None:
                    pe.wait_ge(s_exp, n - 1)
                for kt in range(2):
                    k = slice((2 * kk + kt) * P, (2 * kk + kt + 1) * P)
                    out = sps[:, buf, kt * 512:(kt + 1) * 512]
                    nc.tensor.matmul(out, k_hl[:, par, a, k], q_hh[:, par, a, q], start=True, stop=False)
                    mm = nc.tensor.matmul(out, k_h1[0:HD + 1, par, a, k], q_lm[0:HD + 1, par, a, q],
                                          start=False, stop=True)
                mm.then_inc(s_scores, 1)

            def maxima(par, a, qt, item, pair=None):
                if pair is not None:
                    pe.wait_ge(s_head[a], 96 * pair + 96)
                if item is not None:
                    pe.wait_ge(s_mx, item)
                for kh in range(2):
                    mm = nc.tensor.matmul(mps[:, kh * 512:(kh + 1) * 512], q_hh[:, par, a, qt * P:(qt + 1) * P],
                                          k_hl[:, par, a, kh * 512:(kh + 1) * 512], start=True, stop=True)
                mm.then_inc(s_maxmm, 1)

            def values_of(t):
                for h in range(2):
                    if t >= 2:
                        pe.wait_ge(s_vlo, 2 * (t - 2) + h + 1)
                    nc.tensor.matmul(sps[:, t % 2, h * 512:(h + 1) * 512], xT[:, t * P:(t + 1) * P],
                                     wv[:, h * 512:(h + 1) * 512], start=True, stop=True).then_inc(s_vps, 1)

            def project_early(batch, k, bank):
                x = slice(batch * S + k % 2 * 512, batch * S + k % 2 * 512 + 512)
                nc.tensor.matmul(bank, wqk[:, k // 2, :], xT[:, x], start=True, stop=True).then_inc(s_misc, 1)

            def project(batch, k, job):
                x = slice(batch * S + k % 2 * 512, batch * S + k % 2 * 512 + 512)
                pe.wait_ge(s_used, job)
                nc.tensor.matmul(misc[:], wqk_hi[:, k // 2, :], xT_hi[:, x], start=True, stop=False)
                nc.tensor.matmul(misc[:], wqk_hi[:, k // 2, :], xT_lo[:, x], start=False, stop=False)
                nc.tensor.matmul(misc[:], wqk_lo[:, k // 2, :], xT_hi[:, x], start=False,
                                 stop=True).then_inc(s_misc, 1)

            def turn_maxima(a, job, items):
                pe.wait_ge(s_mx, items)
                pe.wait_ge(s_used, job)
                nc.tensor.transpose(misc[0:TB, 0:P], mx[:, a, :], mem["ident"][:]).then_inc(s_misc, 1)

            def turn_output(par, half, job, units):
                pe.wait_ge(s_oevac, units)
                pe.wait_ge(s_used, job)
                for q in range(4):
                    mm = nc.tensor.transpose(misc[:, q * P:(q + 1) * P], mem["ao"][:, par, 4 * half + q, :],
                                             mem["ident"][:])
                mm.then_inc(s_misc, 1)

            def project_output(par, job, loads):
                pe.wait_ge(s_wo, loads)
                pe.wait_ge(s_used, job)
                for q in range(4):
                    mm = nc.tensor.matmul(misc[:, q * P:(q + 1) * P], aoT[:, q, :], mem["wo"][:, par, :],
                                          start=True, stop=True)
                mm.then_inc(s_misc, 1)

            def values(par, a, c, n, pair):
                half, kk = divmod(c, CH // 2)
                if a == 0 and c == 0:
                    pe.wait_ge(s_v, 16 * pair + 16)
                pe.wait_ge(s_subv, n + 1)
                pe.wait_ge(s_subp, n + 1)
                if kk == 0:
                    pe.wait_ge(s_oevac, 4 * pair + 2 * a + half + 1)
                buf = c % 4
                for kt in range(2):
                    v = vbuf[:, par, 2 * kk + kt, a, :]
                    for q in range(4):
                        w = slice(kt * 512 + q * P, kt * 512 + (q + 1) * P)
                        nc.tensor.matmul(O[:, q, :], ph[:, buf, w], v[:, 0:HD + 1],
                                         start=(kk == 0 and kt == 0 and q == 0), stop=False, skip_group_check=True)
                        nc.tensor.matmul(O[:, q, 0:HD], ph[:, buf, w], v[:, HD + 1:VW],
                                         start=False, stop=False, skip_group_check=True)
                        mm = nc.tensor.matmul(O[:, q, :], pl[:, buf, w], v[:, 0:HD + 1], start=False,
                                              stop=(kk == CH // 2 - 1 and kt == 1 and q == 3), skip_group_check=True)
                mm.then_inc(s_pv, 1)

            pe.wait_ge(s_w, 32)
            pe.wait_ge(s_xT, 16)
            for k in range(4):
                project_early(0, k, p_banks[k])
            pe.wait_ge(s_wv, 16)
            for t in range(T + 2):
                if t < T:
                    values_of(t)
                if P1_TILE <= t < P1_TILE + 4:
                    pe.wait_ge(s_used, 4 + t - P1_TILE)
                    project_early(1, t - P1_TILE, misc[:])
                if t == T + 2 - LEAD_M:
                    pe.wait_ge(s_used, 4)
                    pe.wait_ge(s_ident, 1)
                if t >= T + 2 - LEAD_M:
                    item = t - (T + 2 - LEAD_M)
                    a, qt = divmod(item, TB)
                    maxima(0, a, qt, item, 0 if qt == 0 else None)
                    if item == TB:
                        turn_maxima(0, PRO_MISC - 1, TB)
            pe.wait_ge(s_vlo, 2 * T)
            pe.wait_ge(s_xlo, 1)
            pe.wait_ge(s_init, 1)
            scores(0, 0, 0, None, (0, 0))
            scores(0, 0, 1, None, None)
            scores(0, 0, 2, 2, None)

            def turn_of_pairs(it, last):
                for par in range(2):
                    pp = it * 2 + par
                    jobs, job = jobs_of(last, par), first_job(last, pp, par)
                    for s in range(PCH):
                        n = PCH * pp + s
                        over, t = divmod(s + LEAD_M, PCH)
                        ma, qt = divmod(t, TB)
                        if within(last, par, s + LEAD_M):
                            maxima((par + over) % 2, ma, qt, n + LEAD_M, pp + over if qt == 0 else None)
                        over, t = divmod(s + LEAD_S, PCH)
                        sa, sc = divmod(t, CH)
                        if within(last, par, s + LEAD_S):
                            scores((par + over) % 2, sa, sc, n + LEAD_S,
                                   (pp + over, 2 * (pp + over) + sa) if sc == 0 else None)
                        values(par, s // CH, s % CH, n, pp)
                        if s in jobs:
                            kind, k, number = jobs[s]
                            j = job + number
                            if kind == "turn":
                                turn_output(1 - par, k, j, 4 * pp + 1)
                            if kind == "add":
                                project_output(1 - par, j, 16 * pp + 16)
                            if kind == "maxima":
                                turn_maxima(k, j, PCH * pp + (16 if k else 24))
                            if kind == "project":
                                if par == 0 and k == 0:
                                    pe.wait_ge(s_wlo, it + 1)
                                project(par, k, j)

            with pe.Fori(0, PAIRS // 2 - 1) as it:
                turn_of_pairs(it, False)
            turn_of_pairs(PAIRS // 2 - 1, True)

        @block.scalar
        def _(act):
            def exps(c, n):
                act.wait_ge(s_scores, n + 1)
                buf = q = n if c is None else c
                nc.scalar.activation(p32[:, q % 4, :], sps[:, buf % 2, :], ACT.Exp, bias=EXP_BIAS, scale=SCALE)
                nc.scalar.activation(ph[:, q % 4, :], sps[:, buf % 2, :], ACT.Exp, bias=EXP_BIAS, scale=SCALE).then_inc(s_exp, 1)

            def send_max(par, a, jobs, sent):
                act.wait_ge(s_used, jobs)
                if sent is not None:
                    act.wait_ge(s_negm, sent)
                act.dma_start(q_lm[HD:HD + 1, par, a, :].bitcast(F32),
                              negm[:, a, :].bitcast(F32)).then_inc(s_negm, 16)

            def round_piece(k, job, spread, src=misc[:]):
                if spread is not None and k == 0:
                    for a in range(2):
                        act.wait_ge(s_head[a], spread)
                act.wait_ge(s_misc, job + 1)
                nc.scalar.copy(hi[:, k // 2, k % 2 * 512:(k % 2 + 1) * 512], src).then_inc(s_hi, 1)

            def take_turned(job):
                act.wait_ge(s_misc, job + 1)
                nc.scalar.activation(aoT[:].rearrange("p q t -> p (q t)"), misc[:], ACT.Copy,
                                     scale=vinv[:, 0:1]).then_inc(s_used, 1)

            def round_weights(loads):
                act.wait_ge(s_w, loads)
                nc.scalar.copy(wqk_hi[:], wqk[:]).then_inc(s_whi, 1)

            def high_values(t):
                if t >= V_BUFS:
                    act.wait_ge(s_vout[t % V_BUFS], 16 * (t // V_BUFS))
                for h in range(2):
                    act.wait_ge(s_vps, 2 * t + h + 1)
                    rows = vt[:, t % V_BUFS, h * H // 2:(h + 1) * H // 2, 0:HD]
                    nc.scalar.activation(rows, sps[:, t % 2, h * 512:(h + 1) * 512].rearrange("p (h c) -> p h c", c=HD),
                                         ACT.Copy, scale=vscale[:, 0:1]).then_inc(s_vhi, 1)

            def store_values(t):
                act.wait_ge(s_vlo, 2 * t + 2)
                b, i = divmod(t, TB)
                dst = io["v_dram"][b * H // 2:(b + 1) * H // 2, :, i, :].rearrange("j p c -> p j c")
                act.dma_start(dst, vt[:, t % V_BUFS].rearrange("p (j a) c -> p j (a c)", a=2))\
                    .then_inc(s_vout[t % V_BUFS], 16)

            for k in range(4):
                round_piece(k, k, None, p_banks[k])
            act.wait_ge(s_bound, 3)
            act.wait_ge(s_ones, 1)
            for t in range(T):
                high_values(t)
                if t:
                    store_values(t - 1)
                if P1_TILE <= t < P1_TILE + 4:
                    round_piece(t - P1_TILE, 4 + t - P1_TILE, 96)
                if t == T - 2:
                    send_max(0, 0, PRO_MISC, None)
            store_values(T - 1)
            round_weights(64)
            exps(None, 0)
            exps(None, 1)
            exps(None, 2)
            def turn_of_pairs(it, last):
                for par in range(2):
                    pp = it * 2 + par
                    jobs, job = jobs_of(last, par), first_job(last, pp, par)
                    for s in range(PCH):
                        if within(last, par, s + LEAD_S):
                            exps((s + LEAD_S) % CH, PCH * pp + s + LEAD_S)
                        kind, k, number = jobs.get(s, (None, 0, 0))
                        if kind == "project":
                            round_piece(k, job + number, 96 * pp + 192)
                        if kind == "turn":
                            take_turned(job + number)
                        if par == 1 and s == 8 and not last:
                            round_weights(32 * it + 96)
                        kind, k, number = jobs.get(s - 1, (None, 0, 0))
                        if kind == "maxima":
                            send_max(par if k else 1 - par, k, job + number + 1, 32 * pp + (16 if k else 32))

            with act.Fori(0, PAIRS // 2 - 1) as it:
                turn_of_pairs(it, False)
            turn_of_pairs(PAIRS // 2 - 1, True)
            act.wait_ge(s_negm, 16 * 2 * PAIRS)

        @block.gpsimd
        def _(pool):
            def low_parts(c, n):
                pool.wait_ge(s_exp, n + 1)
                nc.gpsimd.tensor_tensor(pl[:, c % 4, 0:POOL_COLS], p32[:, c % 4, 0:POOL_COLS],
                                        ph[:, c % 4, 0:POOL_COLS], ALU.subtract).then_inc(s_subp, 1)

            nc.gpsimd.memset(mem["ident"][:], 0.0).then_inc(s_zero, 1)
            pool.wait_ge(s_zero, 1)
            nc.gpsimd.affine_select(out=mem["ident"][:], in_=mem["ident"][:], compare_op=ALU.not_equal, fill=1.0,
                                    base=0, pattern=[[-1, P]], channel_multiplier=1).then_inc(s_ident, 1)
            pool.wait_ge(s_top, 2)
            nc.gpsimd.partition_all_reduce(alltops[:], tops[:], P, bass.bass_isa.ReduceOp.max).then_inc(s_alltop, 1)
            nc.gpsimd.memset(mem["ao"][:, 1], 0.0).then_inc(s_oevac, 1)
            pool.wait_ge(s_oevac, 1)
            nc.gpsimd.memset(k_h1[HD:HD + 1].bitcast(F32), 1.0).then_inc(s_init, 1)
            pool.wait_ge(s_init, 1)
            pool.wait_ge(s_x, 16)
            pool.wait_ge(s_bo, 16)
            nc.gpsimd.tensor_tensor(mem["y"][:], mem["y"][:], bo[:].unsqueeze(1).broadcast_to([P, T, D]),
                                    ALU.add).then_inc(s_xbo, 1)
            pool.wait_ge(s_xT, 16)
            nc.gpsimd.tensor_copy(xT_hi[:], xT[:]).then_inc(s_xhi, 1)
            pool.wait_ge(s_xhi, 1)
            nc.gpsimd.tensor_tensor(xT_lo[:], xT[:], xT_hi[:], ALU.subtract).then_inc(s_xlo, 1)
            low_parts(0, 0)
            low_parts(1, 1)
            low_parts(2, 2)
            with pool.Fori(0, PAIRS * PCH // 4 - 1) as it:
                for s in range(4):
                    low_parts(s + LEAD_S, it * 4 + s + LEAD_S)
            for n in range(PAIRS * PCH - 4 + LEAD_S, PAIRS * PCH):
                low_parts(n, n)

        @block.vector
        def _(dve):
            def reduce_max(slot, qt, item):
                dve.wait_ge(s_maxmm, item + 1)
                nc.vector.tensor_reduce(mx[:, slot, qt:qt + 1], mps[:], AX.X, ALU.max).then_inc(s_mx, 1)

            def low_parts(c, n):
                dve.wait_ge(s_exp, n + 1)
                nc.vector.tensor_tensor(pl[:, c % 4, POOL_COLS:], p32[:, c % 4, POOL_COLS:],
                                        ph[:, c % 4, POOL_COLS:], ALU.subtract).then_inc(s_subv, 1)

            def rest_of_weights(n):
                dve.wait_ge(s_whi, n)
                nc.vector.tensor_tensor(wqk_lo[:], wqk[:], wqk_hi[:], ALU.subtract).then_inc(s_wlo, 1)

            def low_values(t):
                for h in range(2):
                    dve.wait_ge(s_vhi, 2 * t + h + 1)
                    rows = vt[:, t % V_BUFS, h * H // 2:(h + 1) * H // 2, :]
                    nc.vector.scalar_tensor_tensor(
                        out=rows[:, :, HD + 1:VW],
                        in0=sps[:, t % 2, h * 512:(h + 1) * 512].rearrange("p (h c) -> p h c", c=HD),
                        scalar=vscale[:, 0:1], in1=rows[:, :, 0:HD], op0=ALU.mult, op1=ALU.subtract).then_inc(s_vlo, 1)

            def rest_of_piece(k, job, pieces, src=misc[:]):
                dve.wait_ge(s_hi, pieces)
                cols = slice(k % 2 * 512, (k % 2 + 1) * 512)
                nc.vector.tensor_tensor(lo[:, k // 2, cols], src, hi[:, k // 2, cols],
                                        ALU.subtract).then_inc(s_used, 1)

            def negate_maxima(a, job, sent):
                if sent is not None:
                    dve.wait_ge(s_negm, sent)
                dve.wait_ge(s_misc, job + 1)
                nc.vector.tensor_scalar(negm[:, a, :], misc[0:TB, 0:P], -1.0, None, ALU.mult).then_inc(s_used, 1)

            def add_output(batch, half, job):
                dve.wait_ge(s_misc, job + 1)
                y = mem["y"][:, batch * TB + 4 * half:batch * TB + 4 * half + 4, :]
                nc.vector.tensor_tensor(y, misc[:].rearrange("p (q d) -> p q d", q=4), y, ALU.add).then_inc(s_used, 1)

            def normalise(par, a, half, unit):
                dve.wait_ge(s_pv, 4 * unit + 4)
                nc.vector.reciprocal(rec[:], O[:, :, HD]).then_inc(s_rec, 1)
                dve.wait_ge(s_rec, unit + 1)
                nc.vector.tensor_tensor(mem["ao"][:, par, 4 * half:4 * half + 4, a * HD:(a + 1) * HD], O[:, :, 0:HD],
                                        rec[:].unsqueeze(2).broadcast_to([P, 4, HD]),
                                        ALU.mult).then_inc(s_oevac, 1)

            nc.vector.memset(vt[:, :, :, HD:HD + 1], 1.0).then_inc(s_ones, 1)
            dve.wait_ge(s_xT, 16)
            nc.vector.tensor_reduce(tops[:, 0:1], xT[:], AX.X, ALU.max, apply_absolute_value=True).then_inc(s_top, 1)
            dve.wait_ge(s_wv, 16)
            nc.vector.tensor_reduce(tops[:, 1:2], wv[:], AX.X, ALU.max, apply_absolute_value=True).then_inc(s_top, 1)
            for k in range(4):
                rest_of_piece(k, k, k + 1, p_banks[k])
            dve.wait_ge(s_alltop, 1)
            nc.vector.scalar_tensor_tensor(out=bound[:], in0=alltops[:, 0:1], scalar=D / V_TOP,
                                           in1=alltops[:, 1:2], op0=ALU.mult, op1=ALU.mult).then_inc(s_bound, 1)
            dve.wait_ge(s_bound, 1)
            nc.vector.tensor_scalar(vinv[:], bound[:], 1e-30, None, ALU.max).then_inc(s_bound, 1)
            dve.wait_ge(s_bound, 2)
            nc.vector.reciprocal(vscale[:], vinv[:]).then_inc(s_bound, 1)
            dve.wait_ge(s_bound, 3)
            dve.wait_ge(s_ones, 1)
            for t in range(T + 2):
                if t < T:
                    low_values(t)
                if P1_TILE <= t < P1_TILE + 4:
                    rest_of_piece(t - P1_TILE, 4 + t - P1_TILE, 5 + t - P1_TILE)
                if t >= T + 2 - LEAD_M:
                    item = t - (T + 2 - LEAD_M)
                    reduce_max(item // TB, item % TB, item)
                    if item == TB:
                        negate_maxima(0, PRO_MISC - 1, None)
            dve.wait_ge(s_xbo, 1)
            rest_of_weights(1)
            low_parts(0, 0)
            def turn_of_pairs(it, last):
                for par in range(2):
                    pp = it * 2 + par
                    jobs, job = jobs_of(last, par), first_job(last, pp, par)
                    for s in range(PCH):
                        n = PCH * pp + s
                        ma, qt = divmod((s + LEAD_M) % PCH, TB)
                        if s in (4, 8, 12):
                            u = s // 4 - 1
                            normalise(par, u // 2, u % 2, 4 * pp + u)
                        kind, k, number = jobs.get(s - 1, (None, 0, 0))
                        if kind == "maxima":
                            negate_maxima(k, job + number, 32 * pp + 16)
                        if kind == "add" and s in JOBS:
                            add_output(1 - par, k, job + number)
                        if within(last, par, s + LEAD_M):
                            reduce_max(ma, qt, n + LEAD_M)
                        if kind == "add" and s not in JOBS:
                            add_output(1 - par, k, job + number)
                        if kind == "project":
                            rest_of_piece(k, job + number, 4 * pp + 9 + k)
                        if par == 1 and s == 9 and not last:
                            rest_of_weights(it + 2)
                        if within(last, par, s + 1):
                            low_parts((s + 1) % CH, n + 1)
                    normalise(par, 1, 1, 4 * pp + 3)

            with dve.Fori(0, PAIRS // 2 - 1) as it:
                turn_of_pairs(it, False)
            turn_of_pairs(PAIRS // 2 - 1, True)


def norm_statistics(nc, k, src, stats, mv, s_var, then):
    tiles = range(4 * k, 4 * k + 4)
    for t in tiles:
        ins = nc.vector.bn_stats(stats[:, t, :], src[:, t, :])
    then(ins)
    for t in tiles:
        ins = nc.vector.bn_aggr(mv[:, t, :], stats[:, t, :])
    then(ins)
    nc.vector.tensor_scalar(mv[:, 4 * k:4 * k + 4, 1:2], mv[:, 4 * k:4 * k + 4, 1:2], EPS, None,
                            ALU.add).then_inc(s_var, 1)


def norm_factors(nc, dve, k, n, mv, rstd, shift, s_root, s_shifted, then):
    g = slice(4 * k, 4 * k + 4)
    dve.wait_ge(s_root, n + 1)
    then(nc.vector.reciprocal(rstd[:, g], rstd[:, g]))
    nc.vector.scalar_tensor_tensor(out=shift[:, g], in0=mv[:, g, 0], scalar=-1.0, in1=rstd[:, g],
                                   op0=ALU.mult, op1=ALU.mult).then_inc(s_shifted, 1)


def norm_root(nc, act, k, n, mv, rstd, s_var, s_root):
    act.wait_ge(s_var, n + 1)
    nc.scalar.activation(rstd[:, 4 * k:4 * k + 4], mv[:, 4 * k:4 * k + 4, 1], ACT.Sqrt).then_inc(s_root, 1)


def norm_apply(nc, act, k, n, src, rstd, shift, s_shifted, s_normed):
    act.wait_ge(s_shifted, n + 1)
    for t in range(4 * k, 4 * k + 4):
        nc.scalar.activation(src[:, t, :], src[:, t, :], ACT.Identity, bias=shift[:, t:t + 1],
                             scale=rstd[:, t:t + 1]).then_inc(s_normed, 1)


def mixture(nc, io, mem):
    BL = T // 4
    NC = len(F_CHUNKS)
    UNITS = BL * 2
    TURNS = E // 2
    STATISTICS, ROOT, FACTORS, APPLY = 1, 2, 3, 4

    def summed_before(steps):
        return [(BL + bl + 1) * NC - 1 + steps for bl in range(BL)]

    with ExitStack() as ctx:
        sb = lambda name, shape, dt: ctx.enter_context(nc.sbuf_tensor(name, shape, dt))
        sem = lambda name: ctx.enter_context(nc.semaphore(name))
        y = mem["y"]
        aoT = sb("aoT2", [P, 2, 512], F32)
        stats = sb("stats", [P, T, 6], F32)
        mv = sb("mv", [P, T, 2], F32)
        rstd = sb("rstd", [P, T], F32)
        shift = sb("shift", [P, T], F32)
        wg = sb("wg", [P, 3 * E], F32)
        mixed = sb("mixed", [P, T, 3 * E], F32)
        prod = sb("prod", [P, T, E, E], F32)
        pv = sb("pv", [P, T, E, E], F32)
        g = sb("g", [P, 9, T, E], F32)
        one = sb("one", [P, 5, T], F32)
        rank = sb("rank", [P, E], F32)
        gate = sb("gate", [P, T, E], F32)
        x1T = sb("x1T", [P, T * P], F32)
        x_hi = sb("x_hi", [P, T * P], F32R)
        x_lo = sb("x_lo", [P, T * P], F32R)
        w1 = sb("w1", [P, 2, 2 * F], F32)
        w1_hi = sb("w1_hi", [P, 2, 2 * F], F32R)
        w1_lo = sb("w1_lo", [P, 2, 2 * F], F32R)
        w2 = sb("w2", [P, 2, NC, D], F32)
        silu = sb("silu", [P, 3, 512], F32)
        he = sb("he", [P, 3, 512], F32)
        part = sb("part", [P, 4, D], F32)
        aps = ctx.enter_context(nc.psum_tensor("aps", [P, 3, 512], F32))
        gps = ctx.enter_context(nc.psum_tensor("gps", [P, 3, 512], F32))
        yps = ctx.enter_context(nc.psum_tensor("yps", [P, 2, 512], F32))
        tps = yps
        mps = gps[:, 2, 0:T * 3 * E]
        s_ao, s_aoT, s_wout = sem("s_ao"), sem("s_aoT"), sem("s_wout")
        s_w = [sem("s_we0"), sem("s_we1")]
        s_wg, s_chain = sem("s_wg"), sem("s_chain")
        s_var, s_root, s_shifted, s_normed = (sem(n) for n in ("s_var", "s_root", "s_shifted", "s_normed"))
        s_turn, s_mixmm, s_mixed = sem("s_turn"), sem("s_mixmm"), sem("s_mixed")
        s_shift, s_gexp, s_out = sem("s_shift"), sem("s_gexp"), sem("s_out")
        s_taken, s_xlo, s_whi, s_wlo = sem("s_taken"), sem("s_xlo"), sem("s_whi"), sem("s_wlo")
        s_h, s_silu, s_he, s_y, s_part, s_add = (sem(n) for n in ("s_h", "s_silu", "s_he", "s_y", "s_part", "s_add"))
        block = ctx.enter_context(nc.Block())

        @block.sync
        def _(sp):
            def ready(x):
                return sp.snap(sp.to_reg(x))

            def load(e, par):
                sp.dma_start(w1[:, par, :], io["w1T"][bass.ds(e, 1), :, :].rearrange("o h f -> h (o f)"))\
                    .then_inc(s_w[par], 16)
                sp.dma_start(w2[:, par, 0:2, :], io["w2T"][bass.ds(e, 1), 0:2 * P, :].rearrange(
                    "o (c p) h -> p (o c) h", p=P)).then_inc(s_w[par], 16)
                sp.dma_start(w2[0:F - 2 * P, par, 2, :], io["w2T"][bass.ds(e, 1), 2 * P:F, :].rearrange(
                    "o p h -> (o p) h")).then_inc(s_w[par], 16)

            sp.dma_start(wg[:], io["wqkvT"]).then_inc(s_wg, 16)
            load(0, 0)
            load(1, 1)
            with sp.Fori(0, TURNS - 1) as it:
                for par in range(2):
                    expert = ready(it * 2 + par + 2)
                    used = ready(it * UNITS + (par + 1) * BL)
                    loaded = ready(it * 48 + 48)
                    sp.wait_ge(s_y, used)
                    sp.wait_ge(s_w[par], loaded)
                    load(expert, par)
            for par in range(2):
                sp.wait_ge(s_w[par], 48 * TURNS)
            out = io["out"].rearrange("b (t p) d -> p (b t) d", p=P)
            for k in range(T // 4):
                sp.wait_ge(s_normed, T + 4 * k + 4)
                sp.dma_start(out[:, 4 * k:4 * k + 4, :], y[:, 4 * k:4 * k + 4, :]).then_inc(s_out, 16)
            sp.wait_ge(s_out, 16 * (T // 4))

        @block.tensor
        def _(pe):
            for half in range(2):
                for q in range(4):
                    tr = nc.tensor.transpose(aps[:, half, q * P:(q + 1) * P], mem["ao"][:, 1, 4 * half + q, :],
                                             mem["ident"][:])
                tr.then_inc(s_ao, 1)
            for half in range(2):
                pe.wait_ge(s_aoT, half + 1)
                for q in range(4):
                    mm = nc.tensor.matmul(gps[:, half, q * D:(q + 1) * D], aoT[:, half, q * P:(q + 1) * P],
                                          mem["wo"][:, 1, :], start=True, stop=True)
                mm.then_inc(s_wout, 1)

            def turn(k):
                if k >= 2:
                    pe.wait_ge(s_taken, k - 1)
                for t in range(4 * k, 4 * k + 4):
                    pe.wait_ge(s_normed, t + 1)
                    tr = nc.tensor.transpose(tps[:, k % 2, t % 4 * P:(t % 4 + 1) * P], y[:, t, :], mem["ident"][:])
                tr.then_inc(s_turn, 1)

            def mix(k):
                pe.wait_ge(s_taken, k + 1)
                for t in range(4 * k, 4 * k + 4):
                    mm = nc.tensor.matmul(mps[:, t * 3 * E:(t + 1) * 3 * E], x1T[:, t * P:(t + 1) * P], wg[:],
                                          start=True, stop=True)
                if k == T // 4 - 1:
                    mm.then_inc(s_mixmm, 1)

            turn(0)
            turn(1)
            pe.wait_ge(s_wg, 16)
            for k in range(T // 4):
                mix(k)
                if k + 2 < T // 4:
                    turn(k + 2)

            def hidden(it, k):
                over, t = divmod(k, UNITS * NC)
                u, c = divmod(t, NC)
                par, bl = divmod(u, BL)
                if bl == 0 and c == 0:
                    pe.wait_ge(s_wlo, (it + over) * 2 + par + 1)
                    pe.wait_ge(s_w[par], (it + over) * 48 + 48)
                off, n = F_CHUNKS[c]
                x = slice(bl * 512, (bl + 1) * 512)
                for out, o in ((aps, off), (gps, F + off)):
                    w = slice(o, o + n)
                    nc.tensor.matmul(out[0:n, t % 3, :], w1_hi[:, par, w], x_hi[:, x], start=True, stop=False)
                    nc.tensor.matmul(out[0:n, t % 3, :], w1_hi[:, par, w], x_lo[:, x], start=False, stop=False)
                    mm = nc.tensor.matmul(out[0:n, t % 3, :], w1_lo[:, par, w], x_hi[:, x], start=False, stop=True)
                mm.then_inc(s_h, 1)

            def down(it, k):
                u, c = divmod(k, NC)
                pe.wait_ge(s_he, it * (UNITS * NC) + k + 1)
                n = F_CHUNKS[c][1]
                for q in range(4):
                    mm = nc.tensor.matmul(yps[:, u % 2, q * D:(q + 1) * D], he[0:n, k % 3, q * P:(q + 1) * P],
                                          w2[0:n, u // BL, c, :], start=(c == 0 and q == 0),
                                          stop=(c == NC - 1 and q == 3), skip_group_check=True)
                if c == NC - 1:
                    mm.then_inc(s_y, 1)

            pe.wait_ge(s_xlo, BL)
            hidden(0, 0)
            hidden(0, 1)
            pe.wait_ge(s_mixed, 1)
            def turn_of_experts(it, last):
                for k in range(UNITS * NC):
                    if not last or k + 2 < UNITS * NC:
                        hidden(it, k + 2)
                    down(it, k)

            with pe.Fori(0, TURNS - 1) as it:
                turn_of_experts(it, False)
            turn_of_experts(TURNS - 1, True)

        @block.scalar
        def _(act):
            def round_w1(par, n):
                act.wait_ge(s_w[par], n)
                nc.scalar.copy(w1_hi[:, par, :], w1[:, par, :]).then_inc(s_whi, 1)

            def take_turned(k):
                cols = slice(k * 512, (k + 1) * 512)
                act.wait_ge(s_turn, k + 1)
                nc.scalar.copy(x1T[:, cols], tps[:, k % 2, :])
                nc.scalar.copy(x_hi[:, cols], tps[:, k % 2, :]).then_inc(s_taken, 1)

            for half in range(2):
                act.wait_ge(s_ao, half + 1)
                nc.scalar.activation(aoT[:, half, :], aps[:, half, :], ACT.Copy,
                                     scale=mem["vinv"][:, 0:1]).then_inc(s_aoT, 1)
            norm_root(nc, act, 0, 0, mv, rstd, s_var, s_root)
            for k in range(T // 4):
                if k + 1 < T // 4:
                    norm_root(nc, act, k + 1, k + 1, mv, rstd, s_var, s_root)
                norm_apply(nc, act, k, k, y, rstd, shift, s_shifted, s_normed)
                if k:
                    take_turned(k - 1)
            take_turned(T // 4 - 1)
            act.wait_ge(s_mixmm, 1)
            nc.scalar.copy(mixed[:].rearrange("p t c -> p (t c)"), mps).then_inc(s_mixed, 1)

            def silus(it, k):
                t = k % (UNITS * NC)
                n = F_CHUNKS[t % NC][1]
                act.wait_ge(s_h, it * (UNITS * NC) + k + 1)
                nc.scalar.activation(silu[0:n, t % 3, :], aps[0:n, t % 3, :], ACT.Silu).then_inc(s_silu, 1)

            silus(0, 0)
            act.wait_ge(s_shift, 1)
            nc.scalar.activation(prod[:], prod[:], ACT.Exp).then_inc(s_gexp, 1)
            silus(0, 1)
            act.wait_ge(s_shift, 2)
            nc.scalar.activation(g[:, 4], g[:, 4], ACT.Exp).then_inc(s_gexp, 1)
            def turn_of_experts(it, last):
                for k in range(UNITS * NC + (APPLY + 1 if last else 0)):
                    if not last or k + 2 < UNITS * NC:
                        silus(it, k + 2)
                    if k == BL // 2 * NC:
                        round_w1(1, it * 48 + 48)
                    if k == (BL + BL // 2) * NC and not last:
                        round_w1(0, it * 48 + 96)
                    if last and k in summed_before(ROOT):
                        bl = summed_before(ROOT).index(k)
                        norm_root(nc, act, bl, BL + bl, mv, rstd, s_var, s_root)
                    if last and k in summed_before(APPLY):
                        bl = summed_before(APPLY).index(k)
                        norm_apply(nc, act, bl, BL + bl, y, rstd, shift, s_shifted, s_normed)

            with act.Fori(0, TURNS - 1) as it:
                turn_of_experts(it, False)
            turn_of_experts(TURNS - 1, True)

        @block.gpsimd
        def _(pool):
            def rest_of_w1(par, n):
                pool.wait_ge(s_whi, n)
                nc.gpsimd.tensor_tensor(w1_lo[:, par, :], w1[:, par, :], w1_hi[:, par, :],
                                        ALU.subtract).then_inc(s_wlo, 1)

            pool.wait_ge(s_w[0], 48)
            nc.gpsimd.tensor_copy(w1_hi[:, 0, :], w1[:, 0, :]).then_inc(s_whi, 1)
            rest_of_w1(0, 1)

            with pool.Fori(0, TURNS - 1) as it:
                rest_of_w1(1, it * 2 + 2)
                rest_of_w1(0, it * 2 + 3)
            rest_of_w1(1, E)

        @block.vector
        def _(dve):
            steps = [0]

            def then(ins):
                steps[0] += 1
                ins.then_inc(s_chain, 1)
                dve.wait_ge(s_chain, steps[0])

            def gated(it, k):
                t = k % (UNITS * NC)
                n = F_CHUNKS[t % NC][1]
                dve.wait_ge(s_silu, it * (UNITS * NC) + k + 1)
                nc.vector.tensor_tensor(he[0:n, t % 3, :], silu[0:n, t % 3, :], gps[0:n, t % 3, :],
                                        ALU.mult).then_inc(s_he, 1)

            def add_unit(it, u):
                par, bl = divmod(u, BL)
                unit = it * UNITS + u
                dve.wait_ge(s_y, unit + 1)
                weight = gate[:, bl * 4:(bl + 1) * 4, bass.ds(it * 2 + par, 1)].broadcast_to([P, 4, D])
                nc.vector.tensor_tensor(part[:], yps[:, u % 2, :].rearrange("p (q d) -> p q d", q=4), weight,
                                        ALU.mult).then_inc(s_part, 1)
                dve.wait_ge(s_part, unit + 1)
                rows = y[:, bl * 4:(bl + 1) * 4, :]
                nc.vector.tensor_tensor(rows, rows, part[:], ALU.add).then_inc(s_add, 1)

            def split_x1(k):
                cols = slice(k * 512, (k + 1) * 512)
                dve.wait_ge(s_taken, k + 1)
                nc.vector.tensor_tensor(x_lo[:, cols], x1T[:, cols], x_hi[:, cols], ALU.subtract).then_inc(s_xlo, 1)

            def add_output(half):
                tiles = slice(TB + 4 * half, TB + 4 * half + 4)
                dve.wait_ge(s_wout, half + 1)
                then(nc.vector.tensor_tensor(y[:, tiles, :], gps[:, half, :].rearrange("p (q d) -> p q d", q=4),
                                             y[:, tiles, :], ALU.add))

            norm_statistics(nc, 0, y, stats, mv, s_var, then)
            for k in range(T // 4):
                if k + 1 < T // 4:
                    if k + 1 >= TB // 4:
                        add_output(k + 1 - TB // 4)
                    norm_statistics(nc, k + 1, y, stats, mv, s_var, then)
                norm_factors(nc, dve, k, k, mv, rstd, shift, s_root, s_shifted, then)
            for k in range(T // 4):
                split_x1(k)
            for e in range(E):
                last = nc.vector.memset(rank[:, e:e + 1], float(E - e))
            then(last)
            q, k, v = (mixed[:, :, i * E:(i + 1) * E] for i in range(3))
            full = [P, T, E, E]
            rows = lambda x: x.unsqueeze(3).broadcast_to(full)
            cols = lambda x: x.unsqueeze(2).broadcast_to(full)
            dve.wait_ge(s_mixed, 1)
            then(nc.vector.tensor_tensor(prod[:], rows(q), cols(k), ALU.mult))
            then(nc.vector.tensor_reduce(g[:, 0], prod[:], AX.X, ALU.max))
            nc.vector.tensor_tensor(prod[:], prod[:], rows(g[:, 0]), ALU.subtract).then_inc(s_shift, 1)
            gated(0, 0)
            dve.wait_ge(s_gexp, 1)
            nc.vector.tensor_tensor(pv[:], prod[:], cols(v), ALU.mult)
            then(nc.vector.tensor_reduce(g[:, 1], prod[:], AX.X, ALU.add))
            nc.vector.tensor_reduce(g[:, 2], pv[:], AX.X, ALU.add)
            then(nc.vector.reciprocal(g[:, 3], g[:, 1]))
            then(nc.vector.tensor_tensor(g[:, 3], g[:, 2], g[:, 3], ALU.mult))
            each = lambda x: x.unsqueeze(2).broadcast_to([P, T, E])
            ranks = rank[:].unsqueeze(1).broadcast_to([P, T, E])
            then(nc.vector.tensor_reduce(one[:, 0, :], g[:, 3], AX.X, ALU.max))
            nc.vector.tensor_tensor(g[:, 4], g[:, 3], each(one[:, 0, :]), ALU.subtract).then_inc(s_shift, 1)

            def largest(logits, top, first, hot, scratch):
                then(nc.vector.tensor_tensor(scratch, logits, each(top), ALU.is_equal))
                then(nc.vector.tensor_tensor(scratch, scratch, ranks, ALU.mult))
                then(nc.vector.tensor_reduce(first, scratch, AX.X, ALU.max))
                then(nc.vector.tensor_tensor(hot, ranks, each(first), ALU.is_equal))

            largest(g[:, 3], one[:, 0, :], one[:, 1, :], g[:, 5], g[:, 6])
            then(nc.vector.scalar_tensor_tensor(out=g[:, 7], in0=g[:, 5], scalar=-3e38, in1=g[:, 3],
                                                op0=ALU.mult, op1=ALU.add))
            gated(0, 1)
            then(nc.vector.tensor_reduce(one[:, 2, :], g[:, 7], AX.X, ALU.max))
            largest(g[:, 7], one[:, 2, :], one[:, 3, :], g[:, 8], g[:, 6])
            then(nc.vector.tensor_tensor(g[:, 5], g[:, 5], g[:, 8], ALU.add))
            dve.wait_ge(s_gexp, 2)
            then(nc.vector.tensor_tensor(g[:, 6], g[:, 4], g[:, 5], ALU.mult))
            then(nc.vector.tensor_reduce(one[:, 4, :], g[:, 6], AX.X, ALU.add))
            then(nc.vector.reciprocal(one[:, 3, :], one[:, 4, :]))
            then(nc.vector.tensor_tensor(gate[:], g[:, 6], each(one[:, 3, :]), ALU.mult))
            def turn_of_experts(it, last):
                for k in range(UNITS * NC + (APPLY + 1 if last else 0)):
                    if not last or k + 2 < UNITS * NC:
                        gated(it, k + 2)
                    if last and k in summed_before(STATISTICS):
                        bl = summed_before(STATISTICS).index(k)
                        dve.wait_ge(s_add, it * UNITS + BL + bl + 1)
                        norm_statistics(nc, bl, y, stats, mv, s_var, then)
                    if last and k in summed_before(FACTORS):
                        bl = summed_before(FACTORS).index(k)
                        norm_factors(nc, dve, bl, BL + bl, mv, rstd, shift, s_root, s_shifted, then)
                    if k % NC == NC - 1 and k < UNITS * NC:
                        add_unit(it, k // NC)

            with dve.Fori(0, TURNS - 1) as it:
                turn_of_experts(it, False)
            turn_of_experts(TURNS - 1, True)


def bass_transformer_layer_moe(nc, x, xT, Wq, Wk, Wv, Wo, bo, wqkvT, w1T, w2T, out):
    io = dict(x=x, xT=xT, Wq=Wq, Wk=Wk, Wv=Wv, Wo=Wo, bo=bo, wqkvT=wqkvT, w1T=w1T, w2T=w2T, out=out)
    io["v_dram"] = nc.dram_tensor("v_dram", [PAIRS, P, TB, 2 * VW], F16, kind="Internal").ap()
    with ExitStack() as ctx:
        sb = lambda name, shape, dt: ctx.enter_context(nc.sbuf_tensor(name, shape, dt))
        mem = {
            "ident": sb("ident", [P, P], F32),
            "y": sb("y", [P, T, D], F32),
            "ao": sb("ao", [P, 2, TB, P], F32),
            "wo": sb("wo", [P, 2, D], F32),
            "vinv": sb("vinv", [P, 1], F32),
        }
        attention(nc, io, mem)
        mixture(nc, io, mem)


def kernel(L0_attn_x, L0_attn_Wq, L0_attn_Wk, L0_attn_Wv, L0_attn_Wo, L0_attn_bo, L0_ffn_wqkv, L0_ffn_w1, L0_ffn_w2):
    import numpy as np
    import concourse.bacc as bacc
    from concourse.bass_utils import run_bass_kernel_spmd

    x = np.ascontiguousarray(L0_attn_x)
    ins = {
        "x": x,
        "xT": np.ascontiguousarray(x.reshape(B * S, D).T),
        "Wq": L0_attn_Wq, "Wk": L0_attn_Wk, "Wv": L0_attn_Wv, "Wo": L0_attn_Wo, "bo": L0_attn_bo,
        "wqkvT": np.ascontiguousarray(np.asarray(L0_ffn_wqkv).T),
        "w1T": np.ascontiguousarray(np.asarray(L0_ffn_w1).transpose(0, 2, 1)),
        "w2T": np.ascontiguousarray(np.asarray(L0_ffn_w2).transpose(0, 2, 1)),
    }
    nc = bacc.Bacc("TRN2", target_bir_lowering=False, num_devices=1)
    arrays, args = {}, []
    for name, a in ins.items():
        a = np.ascontiguousarray(a)
        arrays[f"in_{name}"] = a
        args.append(nc.dram_tensor(f"in_{name}", a.shape, mybir.dt.from_np(a.dtype), kind="ExternalInput").ap())
    args.append(nc.dram_tensor("out_0", (B, S, D), F32, kind="ExternalOutput").ap())
    bass_transformer_layer_moe(nc, *args)
    r = run_bass_kernel_spmd(nc, [arrays], core_ids=[0])
    return r.results[0]["out_0"]
```
